# Optimizing a Trainium2 kernel written in Bass

```python
import numpy as np
import jax
import jax.numpy as jnp

def _softmax(x, axis=-1):
    return jax.nn.softmax(x, axis=axis)

def _gelu(x):
    return jax.nn.gelu(x, approximate=True)

def _silu(x):
    return jax.nn.silu(x)

def _sigmoid(x):
    return jax.nn.sigmoid(x)

def _layernorm(x, axis=-1, eps=1e-05):
    m = jnp.mean(x, axis=axis, keepdims=True)
    v = jnp.var(x, axis=axis, keepdims=True)
    return (x - m) / jnp.sqrt(v + eps)

def _scatter_add(tgt, idx, src, axis=0):
    return tgt.at[idx].add(src)

def _segment_sum(src, seg, n):
    return jax.ops.segment_sum(src, seg, n)
kernel_name = 'mk_adj_resnorm_d1_adj_r2_a54619'

def setup_inputs(seed: int=0):
    np.random.seed(seed)
    _w = jnp.asarray

    def _rec_inputs():
        import jax
        import jax.numpy as jnp
        _gk = jax.random.key(seed)
        x = -0.0001538 + 1 * jax.random.normal(jax.random.fold_in(_gk, 1), (32, 256, 384), jnp.float32)
        _a = jax.random.bernoulli(jax.random.fold_in(_gk, 2), 0.0625, (32, 256, 256))
        _a = jnp.logical_or(_a, jnp.swapaxes(_a, -1, -2))
        _a = jnp.logical_or(_a, jnp.eye(256, dtype=bool))
        adj = _a
        return (x, adj)
    x, adj = _rec_inputs()

    def _L0_gnn_setup():
        import jax, jax.numpy as jnp
        import numpy as np
        B, S, H = (4, 1024, 384)
        NUM_HEADS = 6
        HEAD_SIZE = H // NUM_HEADS
        NEG = -9000000000000000.0

        def _heads(x):
            b, s, _ = x.shape
            return x.reshape(b, s, NUM_HEADS, HEAD_SIZE).transpose(0, 2, 1, 3)
        key = jax.random.key(seed)
        ks = jax.random.split(key, 10)
        seq_inputs = jax.random.normal(ks[0], (B, S, H), dtype=jnp.float32)
        gm = jax.random.randint(ks[1], (B, S, S), 0, 2) > 0
        graph_mask = gm | jnp.eye(S, dtype=bool)[None]
        sc = 1.0 / np.sqrt(H)
        Wq = jax.random.normal(ks[2], (H, H), dtype=jnp.float32) * sc
        bq = jnp.zeros((H,), dtype=jnp.float32)
        Wk = jax.random.normal(ks[3], (H, H), dtype=jnp.float32) * sc
        bk = jnp.zeros((H,), dtype=jnp.float32)
        Wv = jax.random.normal(ks[4], (H, H), dtype=jnp.float32) * sc
        bv = jnp.zeros((H,), dtype=jnp.float32)
        Wf = jax.random.normal(ks[5], (H, H), dtype=jnp.float32) * sc
        bf = jnp.zeros((H,), dtype=jnp.float32)
        return {'seq_inputs': seq_inputs, 'Wq': Wq, 'bq': bq, 'Wk': Wk, 'bk': bk, 'Wv': Wv, 'bv': bv, 'Wf': Wf, 'bf': bf, 'graph_mask': graph_mask}
    _L0_gnn_all = _L0_gnn_setup()
    _L0_gnn_in = {k: v for k, v in _L0_gnn_all.items() if k in ('Wq', 'bq', 'Wk', 'bk', 'Wv', 'bv', 'Wf', 'bf')}
    del _L0_gnn_all
    return {'x': x, 'adj': adj, 'L0_gnn_Wq': _L0_gnn_in['Wq'], 'L0_gnn_bq': _L0_gnn_in['bq'], 'L0_gnn_Wk': _L0_gnn_in['Wk'], 'L0_gnn_bk': _L0_gnn_in['bk'], 'L0_gnn_Wv': _L0_gnn_in['Wv'], 'L0_gnn_bv': _L0_gnn_in['bv'], 'L0_gnn_Wf': _L0_gnn_in['Wf'], 'L0_gnn_bf': _L0_gnn_in['bf']}

def reference(x, adj, L0_gnn_Wq, L0_gnn_bq, L0_gnn_Wk, L0_gnn_bk, L0_gnn_Wv, L0_gnn_bv, L0_gnn_Wf, L0_gnn_bf):
    import jax
    import jax.numpy as jnp

    def _L0_gnn_ref(seq_inputs, Wq, bq, Wk, bk, Wv, bv, Wf, bf, graph_mask):
        import jax, jax.numpy as jnp
        import numpy as np
        B, S, H = (4, 1024, 384)
        NUM_HEADS = 6
        HEAD_SIZE = H // NUM_HEADS
        NEG = -9000000000000000.0

        def _heads(x):
            b, s, _ = x.shape
            return x.reshape(b, s, NUM_HEADS, HEAD_SIZE).transpose(0, 2, 1, 3)
        q = _heads(seq_inputs @ Wq + bq)
        k = _heads(seq_inputs @ Wk + bk)
        v = _heads(seq_inputs @ Wv + bv)
        scores = jnp.einsum('bhqd,bhkd->bhqk', q, k) / np.sqrt(HEAD_SIZE)
        bias = jnp.where(graph_mask, 0.0, NEG)[:, None]
        probs = jax.nn.softmax(scores + bias, axis=-1)
        ctx = jnp.einsum('bhqk,bhkd->bhqd', probs, v)
        ctx = ctx.transpose(0, 2, 1, 3).reshape(seq_inputs.shape[0], seq_inputs.shape[1], H)
        return ctx @ Wf + bf
    x = _layernorm(x + _L0_gnn_ref(x, L0_gnn_Wq, L0_gnn_bq, L0_gnn_Wk, L0_gnn_bk, L0_gnn_Wv, L0_gnn_bv, L0_gnn_Wf, L0_gnn_bf, adj), axis=-1)
    return x

_drawn_inputs = setup_inputs


def setup_inputs(seed=0):
    import zlib

    import numpy as np

    out = dict(_drawn_inputs(seed))
    spreads = {'L0_gnn_bq': (0.0, 0.34),
     'L0_gnn_bk': (0.0, 0.8),
     'L0_gnn_bv': (0.0, 0.1),
     'L0_gnn_bf': (0.0, 0.1)}
    factors = {}
    for name, (base, spread) in spreads.items():
        noise = np.random.default_rng([zlib.crc32(name.encode()), seed]).standard_normal(out[name].shape)
        drawn = base * np.exp(spread * noise) if base else spread * noise
        out[name] = jnp.asarray(drawn.astype(out[name].dtype))
    for name, factor in factors.items():
        out[name] = (out[name] * factor).astype(out[name].dtype)
    return out
```

```python
from contextlib import ExitStack

import concourse.bass as bass
from concourse import mybir

F32 = mybir.dt.float32
F32R = mybir.dt.float32r
U8 = mybir.dt.uint8
ALU = mybir.AluOpType
ACT = mybir.ActivationFunctionType

P = 128
NEG = -9000000000000000.0
EPS = 1e-05
SMALLEST_START = 3.0e38


class Pair:

    def __init__(self, m, off):
        self.m, self.off, self.par = m, off, off % 2

    def plus(self, d):
        return Pair(self.m, self.off + d)

    def number(self):
        return self.m * 2 + self.off

    def count(self, per, k):
        return self.m * (2 * per) + (self.off * per + k)

    def dma(self):
        return self.m * 16 + (self.off // 2 * 16 + 16)


def wait(eng, sem, value):
    if not isinstance(value, int) or value > 0:
        eng.wait_ge(sem, value)


def hold(eng, sem, value):
    if not isinstance(value, int):
        eng.wait_ge(sem, value)
        eng.nop(nofuse=True)
    elif value > 0:
        eng.wait_ge(sem, value)


def graph_attention(nc, x, adj, wq, bq, wk, bk, wv, bv, wf, bf, out):
    B, S, D = x.shape
    H = 6
    HD = D // H
    C = D // P
    QT = S // P
    T = 2 * QT
    N = T * P
    PAIRS = B // 2
    UNITS = 2 * C
    TILES = 2 * QT
    SCALE = float(HD) ** -0.5
    assert HD == 64 and QT == 2 and C == 3 and PAIRS % 2 == 0 and PAIRS >= 6

    x_rows = x.rearrange("b s d -> (b s) d").rearrange("(j t p) d -> j p t d", t=T, p=P)
    out_rows = out.rearrange("b s d -> (b s) d").rearrange("(j t p) d -> j p t d", t=T, p=P)
    adj_rows = adj.rearrange("b s k -> (b s) k").rearrange("(j t p) k -> j p t k", t=T, p=P)
    weights = [w.rearrange("(c p) n -> p c n", p=P) for w in (wq, wk, wv, wf)]
    WQ, WK, WV, WF = range(4)

    WORK = [
        [("q", 0, 0), ("k", 0, 1)],
        [("q", 1, 0), ("k", 1, 1), ("v", 0, 0)],
        [("q", 2, 1), ("k", 2, 0)],
        [("v", 1, 1), ("v", 2, 0), ("v", 3, 1)],
        [("x", 0, 0), ("o", 0, 1), ("x", 1, 0), ("o", 1, 1)],
        [("x", 2, 0), ("o", 2, 1), ("o", 3, 0)],
    ]
    FIRST = [("x", 0, 0, 0), ("x", 0, 1, 1), ("x", 0, 2, 0),
             ("q", 0, 0, 1), ("k", 0, 0, 0), ("q", 0, 1, 1), ("k", 0, 1, 0), ("q", 0, 2, 1), ("k", 0, 2, 0),
             ("v", 0, 0, 1), ("v", 0, 1, 0), ("v", 0, 2, 1), ("v", 0, 3, 0),
             ("x", 1, 0, 1), ("x", 1, 1, 0), ("x", 1, 2, 1)]
    AHEAD = {"q": 1, "k": 1, "v": 1, "x": 2, "o": -1}

    def work(i, u):
        for kind, n, bank in WORK[u]:
            j = i.plus(AHEAD[kind])
            if not isinstance(i.m, int) or 0 <= j.off < PAIRS:
                yield kind, j, n, bank

    def turns(eng, turn):
        turn(Pair(0, 0))
        turn(Pair(0, 1))
        with eng.Fori(1, PAIRS // 2 - 1) as m:
            turn(Pair(m, 0))
            turn(Pair(m, 1))
        turn(Pair(0, PAIRS - 2))
        turn(Pair(0, PAIRS - 1))

    with ExitStack() as ctx:
        def sb(name, shape, dt):
            return ctx.enter_context(nc.sbuf_tensor(name, shape, dt))

        def psum(name):
            return ctx.enter_context(nc.psum_tensor(name, [P, 512], F32))

        def sem(name):
            return ctx.enter_context(nc.semaphore(name))

        ident = sb("ident", [P, P], F32)
        neg_half = sb("neg_half", [P, T], F32)
        bq_col = sb("bq_col", [P, C], F32)
        bk_col = sb("bk_col", [P, C], F32)
        bv_col = sb("bv_col", [P, C], F32)
        bf_row = sb("bf_row", [P, D], F32)
        w_raw = sb("w_raw", [P, 2, C, D], F32)
        w_high = sb("w_high", [P, 4, C, D], F32R)
        w_low = sb("w_low", [P, 4, C, D], F32R)
        x_raw = sb("x_raw", [P, 2, T, D], F32)
        xt_high = sb("xt_high", [P, C, N], F32R)
        xt_low = sb("xt_low", [P, C, N], F32R)
        qk_high = sb("qk_high", [P, 2, 2, C, N], F32R)
        qk_low = sb("qk_low", [P, 2, 2, C, N], F32R)
        v_sb = sb("v_sb", [P, 2, T, D], F32)
        adj_raw = sb("adj_raw", [P, 2, T, S], U8)
        mask = sb("mask", [P, 2, T, S], F32)
        probs = sb("probs", [P, 2, TILES, S], F32)
        low_col = sb("low_col", [P, UNITS * TILES], F32)
        sum_col = sb("sum_col", [P, UNITS * TILES], F32)
        inv_col = sb("inv_col", [P, UNITS * TILES], F32)
        probs_t = sb("probs_t", [P, 2, 2, 512], F32)
        ctx_high = sb("ctx_high", [P, 2, C, N], F32R)
        ctx_low = sb("ctx_low", [P, 2, C, N], F32R)
        resid = sb("resid", [P, T, D], F32)
        y_sb = sb("y_sb", [P, 2, T, D], F32)
        stats = sb("stats", [P, T, 6], F32)
        mean_var = sb("mean_var", [P, T, 2], F32)
        var_eps = sb("var_eps", [P, T], F32)
        rstd = sb("rstd", [P, T], F32)

        score_bank = [psum(f"score_bank{n}") for n in range(3)]
        turned_bank = [psum(f"turned_bank{n}") for n in range(2)]
        ctx_bank = psum("ctx_bank")
        proj_bank = [psum(f"proj_bank{n}") for n in range(2)]

        x_loaded = [sem(f"x_loaded{n}") for n in range(2)]
        adj_loaded = [sem(f"adj_loaded{n}") for n in range(2)]
        w_loaded = [sem(f"w_loaded{n}") for n in range(4)]
        bias_loaded = sem("bias_loaded")
        resid_loaded = sem("resid_loaded")
        out_stored = [sem(f"out_stored{n}") for n in range(2)]
        ident_zero = sem("ident_zero")
        const_ready = sem("const_ready")
        w_high_ready = sem("w_high_ready")
        w_ready = sem("w_ready")
        x_turned = sem("x_turned")
        xt_high_ready = sem("xt_high_ready")
        xt_ready = sem("xt_ready")
        qk_done = sem("qk_done")
        qk_high_ready = sem("qk_high_ready")
        qk_ready = sem("qk_ready")
        v_done = sem("v_done")
        v_ready = sem("v_ready")
        o_done = sem("o_done")
        y_ready = sem("y_ready")
        mask_built = sem("mask_built")
        scores_done = sem("scores_done")
        masked = sem("masked")
        exp_done = sem("exp_done")
        inv_ready = sem("inv_ready")
        scaled = sem("scaled")
        p_turned = sem("p_turned")
        pt_ready = sem("pt_ready")
        pv_done = sem("pv_done")
        ctx_high_ready = sem("ctx_high_ready")
        ctx_ready = sem("ctx_ready")
        resid_ready = sem("resid_ready")
        stats_ready = sem("stats_ready")
        var_ready = sem("var_ready")
        eps_added = sem("eps_added")
        rstd_ready = sem("rstd_ready")
        normed = sem("normed")

        def emptied(kind, j, n):
            return {"x": (xt_ready, j.count(C, n + 1)), "q": (qk_ready, j.count(2 * C, 2 * n + 1)),
                    "k": (qk_ready, j.count(2 * C, 2 * n + 2)), "v": (v_ready, j.count(T, n + 1)),
                    "o": (y_ready, j.count(T, n + 1))}[kind]

        block = ctx.enter_context(nc.Block())

        @block.sync
        def _(sp):
            def load_x(j):
                hold(sp, x_turned, j.plus(-2).count(C, C))
                sp.dma_start(x_raw[:, j.par], x_rows[j.number()]).then_inc(x_loaded[j.par], 16)

            def load_adj(j):
                hold(sp, mask_built, j.plus(-2).count(2, 2))
                sp.dma_start(adj_raw[:, j.par], adj_rows[j.number()]).then_inc(adj_loaded[j.par], 16)

            def load_resid(j):
                hold(sp, y_ready, j.plus(-1).count(T, T))
                sp.dma_start(resid[:], x_rows[j.number()]).then_inc(resid_loaded, 16)

            def store(j):
                hold(sp, normed, j.count(T, T))
                sp.dma_start(out_rows[j.number()], y_sb[:, j.par]).then_inc(out_stored[j.par], 16)

            def turn(i):
                peeled = isinstance(i.m, int)
                if not peeled or i.off + 2 < PAIRS:
                    load_x(i.plus(2))
                if not peeled or i.off + 1 < PAIRS:
                    load_adj(i.plus(1))
                if not peeled or i.off >= 1:
                    load_resid(i.plus(-1))
                if not peeled or i.off >= 2:
                    store(i.plus(-2))

            load_x(Pair(0, 0))
            for n in (WQ, WK):
                sp.dma_start(w_raw[:, n % 2], weights[n]).then_inc(w_loaded[n], 16)
            for column, bias in ((bq_col, bq), (bk_col, bk), (bv_col, bv)):
                sp.dma_start(column[:], bias.rearrange("(c p) -> p c", p=P),
                             allow_slow_non_contiguous=True).then_inc(bias_loaded, 16)
            sp.dma_start(bf_row[:], bf.partition_broadcast(P)).then_inc(bias_loaded, 16)
            load_x(Pair(0, 1))
            load_adj(Pair(0, 0))
            for n in (WV, WF):
                sp.wait_ge(w_ready, n - 1)
                sp.dma_start(w_raw[:, n % 2], weights[n]).then_inc(w_loaded[n], 16)
            turns(sp, turn)
            load_resid(Pair(0, PAIRS - 1))
            store(Pair(0, PAIRS - 2))
            store(Pair(0, PAIRS - 1))
            for par in range(2):
                sp.wait_ge(out_stored[par], 16 * (PAIRS // 2))

        @block.gpsimd
        def _(pool):
            def build_mask(j, g):
                hold(pool, masked, j.plus(-2).count(UNITS * TILES, UNITS * TILES))
                if g == 0:
                    hold(pool, adj_loaded[j.par], j.dma())
                rows = slice(g * QT, (g + 1) * QT)
                nc.gpsimd.tensor_scalar(mask[:, j.par, rows], adj_raw[:, j.par, rows], -NEG / SCALE, NEG / SCALE,
                                        ALU.mult, ALU.add).then_inc(mask_built, 1)

            def scale_probs(i, u):
                hold(pool, inv_ready, i.count(UNITS, u + 1))
                for k in range(TILES):
                    tile = probs[:, u % 2, k]
                    at = u * TILES + k
                    nc.gpsimd.tensor_scalar(tile, tile, inv_col[:, at:at + 1], 1.0, ALU.mult,
                                            ALU.mult).then_inc(scaled, 1)

            def add_bias(j, t):
                if t == 0:
                    pool.wait_ge(resid_loaded, j.m * 32 + (j.off * 16 + 16))
                nc.gpsimd.tensor_tensor(resid[:, t], resid[:, t], bf_row[:], ALU.add).then_inc(resid_ready, 1)

            def make_rstd(j):
                hold(pool, var_ready, j.count(T, T))
                nc.gpsimd.tensor_scalar(var_eps[:], mean_var[:, :, 1], EPS, None, ALU.add).then_inc(eps_added, 1)
                hold(pool, eps_added, j.count(1, 1))
                nc.gpsimd.tensor_tensor(rstd[:], var_eps[:], neg_half[:], ALU.pow).then_inc(rstd_ready, 1)

            def turn(i):
                peeled = isinstance(i.m, int)
                for u in range(UNITS):
                    scale_probs(i, u)
                    if u < 2 and (not peeled or i.off + 1 < PAIRS):
                        build_mask(i.plus(1), u)
                    if u == 1 and (not peeled or i.off >= 2):
                        make_rstd(i.plus(-2))
                    if u in (2, 3) and (not peeled or i.off >= 1):
                        add_bias(i.plus(-1), 2 * u - 4)
                        add_bias(i.plus(-1), 2 * u - 3)

            nc.gpsimd.memset(ident[:], 0.0).then_inc(ident_zero, 1)
            nc.gpsimd.memset(neg_half[:], -0.5).then_inc(const_ready, 1)
            pool.wait_ge(ident_zero, 1)
            nc.gpsimd.affine_select(out=ident[:], in_=ident[:], compare_op=ALU.not_equal, fill=1.0, base=0,
                                    pattern=[[-1, P]], channel_multiplier=1).then_inc(const_ready, 1)
            pool.wait_ge(const_ready, 2)
            for g in range(2):
                build_mask(Pair(0, 0), g)
            pool.wait_ge(bias_loaded, 64)
            turns(pool, turn)
            make_rstd(Pair(0, PAIRS - 2))
            for t in range(T):
                add_bias(Pair(0, PAIRS - 1), t)
            make_rstd(Pair(0, PAIRS - 1))

        @block.scalar
        def _(act):
            def split_weight(n):
                act.wait_ge(w_loaded[n], 16)
                nc.scalar.copy(w_high[:, n], w_raw[:, n % 2]).then_inc(w_high_ready, 1)

            def exps(i, u):
                for k in range(TILES):
                    at = u * TILES + k
                    act.wait_ge(masked, i.count(UNITS * TILES, at + 1))
                    tile = probs[:, u % 2, k]
                    nc.scalar.activation(tile, tile, ACT.Exp, bias=low_col[:, at:at + 1], scale=-1.0,
                                         accum_out=sum_col[:, at:at + 1]).then_inc(exp_done, 1)

            def copy_turned(i, u):
                wait(act, pv_done, i.count(UNITS, u - 1))
                for h in range(2):
                    act.wait_ge(p_turned, i.count(2 * UNITS, 2 * u + h + 1))
                    nc.scalar.copy(probs_t[:, u % 2, h], turned_bank[h][:]).then_inc(pt_ready, 1)

            def context_high(i, c):
                act.wait_ge(pv_done, i.count(UNITS, 2 * c + 2))
                nc.scalar.activation(ctx_high[:, i.par, c], ctx_bank[:], ACT.Identity,
                                     bias=bv_col[:, c:c + 1]).then_inc(ctx_high_ready, 1)

            def take(kind, j, n, bank):
                if kind == "x":
                    act.wait_ge(x_turned, j.count(C, n + 1))
                    nc.scalar.copy(xt_high[:, n], proj_bank[bank][:]).then_inc(xt_high_ready, 1)
                elif kind in "qk":
                    which = "qk".index(kind)
                    act.wait_ge(qk_done, j.count(2 * C, 2 * n + which + 1))
                    nc.scalar.activation(qk_high[:, j.par, which, n], proj_bank[bank][:], ACT.Identity,
                                         bias=(bq_col, bk_col)[which][:, n:n + 1]).then_inc(qk_high_ready, 1)
                elif kind == "v":
                    act.wait_ge(v_done, j.count(T, n + 1))
                    nc.scalar.copy(v_sb[:, j.par, n], proj_bank[bank][:, 0:D]).then_inc(v_ready, 1)

            def turn(i):
                for u in range(UNITS):
                    exps(i, u)
                    if u or not (isinstance(i.m, int) and i.off == 0):
                        before = (i, u - 1) if u else (i.plus(-1), UNITS - 1)
                        copy_turned(*before)
                    if u in (3, 5):
                        context_high(i, u // 2 - 1)
                    if u == 1 and not (isinstance(i.m, int) and i.off == 0):
                        context_high(i.plus(-1), C - 1)
                    for kind, j, n, bank in work(i, u):
                        take(kind, j, n, bank)

            split_weight(WQ)
            for kind, j, n, bank in FIRST[:3]:
                take(kind, Pair(0, j), n, bank)
            split_weight(WK)
            act.wait_ge(bias_loaded, 64)
            for kind, j, n, bank in FIRST[3:9]:
                take(kind, Pair(0, j), n, bank)
            split_weight(WV)
            for kind, j, n, bank in FIRST[9:]:
                take(kind, Pair(0, j), n, bank)
            split_weight(WF)
            turns(act, turn)
            copy_turned(Pair(0, PAIRS - 1), UNITS - 1)
            context_high(Pair(0, PAIRS - 1), C - 1)

        @block.vector
        def _(dve):
            def split_weight(n):
                dve.wait_ge(w_high_ready, n + 1)
                nc.vector.tensor_tensor(w_low[:, n], w_raw[:, n % 2], w_high[:, n].bitcast(F32),
                                        ALU.subtract).then_inc(w_ready, 1)

            def mask_scores(i, u):
                if u == 0:
                    hold(dve, mask_built, i.count(2, 2))
                hold(dve, p_turned, i.count(2 * UNITS, 2 * (u - 1)))
                for k in range(TILES):
                    h, q = k // QT, k % QT
                    at = u * TILES + k
                    if q == 0:
                        hold(dve, scores_done, i.count(2 * UNITS, 2 * u + h + 1))
                    nc.vector.tensor_tensor_reduce(
                        out=probs[:, u % 2, k], in0=score_bank[(2 * u + h) % 3][:, q * S:(q + 1) * S],
                        in1=mask[:, i.par, (u % 2) * QT + q], scale=-SCALE, scalar=SMALLEST_START, op0=ALU.add,
                        op1=ALU.min, accum_out=low_col[:, at:at + 1]).then_inc(masked, 1)

            def invert_sums(i, u):
                dve.wait_ge(exp_done, i.count(UNITS * TILES, (u + 1) * TILES))
                cols = slice(u * TILES, (u + 1) * TILES)
                nc.vector.reciprocal(inv_col[:, cols], sum_col[:, cols]).then_inc(inv_ready, 1)

            def context_low(i, c):
                dve.wait_ge(ctx_high_ready, i.count(C, c + 1))
                nc.vector.scalar_tensor_tensor(out=ctx_low[:, i.par, c], in0=ctx_bank[:], scalar=bv_col[:, c:c + 1],
                                               in1=ctx_high[:, i.par, c].bitcast(F32), op0=ALU.add,
                                               op1=ALU.subtract).then_inc(ctx_ready, 1)

            def take(kind, j, n, bank):
                if kind == "x":
                    dve.wait_ge(xt_high_ready, j.count(C, n + 1))
                    nc.vector.tensor_tensor(xt_low[:, n], proj_bank[bank][:], xt_high[:, n].bitcast(F32),
                                            ALU.subtract).then_inc(xt_ready, 1)
                elif kind in "qk":
                    which = "qk".index(kind)
                    dve.wait_ge(qk_high_ready, j.count(2 * C, 2 * n + which + 1))
                    nc.vector.scalar_tensor_tensor(
                        out=qk_low[:, j.par, which, n], in0=proj_bank[bank][:],
                        scalar=(bq_col, bk_col)[which][:, n:n + 1], in1=qk_high[:, j.par, which, n].bitcast(F32),
                        op0=ALU.add, op1=ALU.subtract).then_inc(qk_ready, 1)
                elif kind == "o":
                    if n == 0:
                        wait(dve, out_stored[j.par], j.plus(-2).dma())
                    dve.wait_ge(resid_ready, j.count(T, n + 1))
                    dve.wait_ge(o_done, j.count(T, n + 1))
                    nc.vector.tensor_tensor(y_sb[:, j.par, n], proj_bank[bank][:, 0:D], resid[:, n],
                                            ALU.add).then_inc(y_ready, 1)

            def moments(j):
                dve.wait_ge(y_ready, j.count(T, T))
                for t in range(T):
                    nc.vector.bn_stats(stats[:, t], y_sb[:, j.par, t]).then_inc(stats_ready, 1)
                for t in range(T):
                    hold(dve, stats_ready, j.count(T, t + 1))
                    nc.vector.bn_aggr(mean_var[:, t], stats[:, t]).then_inc(var_ready, 1)

            def normalise(j):
                dve.wait_ge(rstd_ready, j.count(1, 1))
                for t in range(T):
                    nc.vector.tensor_scalar(y_sb[:, j.par, t], y_sb[:, j.par, t], mean_var[:, t, 0:1],
                                            rstd[:, t:t + 1], ALU.subtract, ALU.mult).then_inc(normed, 1)

            def turn(i):
                peeled = isinstance(i.m, int)
                for u in range(UNITS):
                    mask_scores(i, u)
                    if u in (3, 5):
                        context_low(i, u // 2 - 1)
                    if u == 1 and (not peeled or i.off >= 1):
                        context_low(i.plus(-1), C - 1)
                    invert_sums(i, u)
                    for kind, j, n, bank in work(i, u):
                        take(kind, j, n, bank)
                    if u == 0 and (not peeled or i.off >= 2):
                        moments(i.plus(-2))
                    if u == 2 and (not peeled or i.off >= 2):
                        normalise(i.plus(-2))

            split_weight(WQ)
            for kind, j, n, bank in FIRST[:3]:
                take(kind, Pair(0, j), n, bank)
            split_weight(WK)
            for kind, j, n, bank in FIRST[3:9]:
                take(kind, Pair(0, j), n, bank)
            split_weight(WV)
            for kind, j, n, bank in FIRST[9:]:
                take(kind, Pair(0, j), n, bank)
            split_weight(WF)
            turns(dve, turn)
            last = Pair(0, PAIRS - 1)
            moments(last.plus(-1))
            context_low(last, C - 1)
            normalise(last.plus(-1))
            for t in range(T):
                take("o", last, t, t % 2)
            moments(last)
            normalise(last)

        @block.tensor
        def _(pe):
            def split_product(bank_ap, terms):
                for n, (stationary, moving) in enumerate(terms):
                    last = nc.tensor.matmul(bank_ap, stationary, moving, start=(n == 0), stop=(n == len(terms) - 1))
                return last

            def scores(i, u):
                c, g = u // 2, u % 2
                banks = [score_bank[(2 * u + h) % 3] for h in range(2)]
                if g == 0:
                    pe.wait_ge(qk_ready, i.count(2 * C, 2 * c + 2))
                wait(pe, masked, i.count(UNITS * TILES, 2 * (2 * u + 1) - 4))
                keys = slice(g * S, (g + 1) * S)
                for q in range(QT):
                    rows = slice(g * S + q * P, g * S + (q + 1) * P)
                    for n, (q_part, k_part) in enumerate(((qk_low, qk_high), (qk_high, qk_low), (qk_high, qk_high))):
                        for h in range(2):
                            d = slice(h * HD, (h + 1) * HD)
                            mm = nc.tensor.matmul(banks[h][:, q * S:(q + 1) * S], q_part[d, i.par, 0, c, rows],
                                                  k_part[d, i.par, 1, c, keys], start=(n == 0), stop=(n == 2))
                            if q == QT - 1 and n == 2:
                                mm.then_inc(scores_done, 1)

            def turn_probs(i, u):
                for h in range(2):
                    pe.wait_ge(scaled, i.count(UNITS * TILES, u * TILES + (h + 1) * QT))
                    wait(pe, pt_ready, i.count(2 * UNITS, 2 * (u - 1) + h + 1))
                    for q in range(QT):
                        for k in range(QT):
                            at = k * S + q * P
                            mm = nc.tensor.transpose(turned_bank[h][:, at:at + P],
                                                     probs[:, u % 2, h * QT + q, k * P:(k + 1) * P], ident[:])
                    mm.then_inc(p_turned, 1)

            def times_v(i, u):
                c, g = u // 2, u % 2
                if u == 0:
                    pe.wait_ge(v_ready, i.count(T, T))
                if g == 0:
                    wait(pe, ctx_ready, i.count(C, c))
                pe.wait_ge(pt_ready, i.count(2 * UNITS, 2 * u + 2))
                for k in range(QT):
                    for h in range(2):
                        d = slice(h * HD, (h + 1) * HD)
                        feats = slice(c * P + h * HD, c * P + (h + 1) * HD)
                        mm = nc.tensor.matmul(ctx_bank[d, g * S:(g + 1) * S], v_sb[:, i.par, g * QT + k, feats],
                                              probs_t[:, u % 2, h, k * S:(k + 1) * S],
                                              start=(k == 0), stop=(k == QT - 1))
                mm.then_inc(pv_done, 1)

            def make(kind, j, n, bank):
                full = proj_bank[bank][:]
                tokens = slice(n * P, (n + 1) * P)
                if kind == "x":
                    if n == 0:
                        pe.wait_ge(x_loaded[j.par], j.dma())
                    for t in range(T):
                        mm = nc.tensor.transpose(full[:, t * P:(t + 1) * P], x_raw[:, j.par, t, tokens], ident[:])
                    mm.then_inc(x_turned, 1)
                elif kind in "qk":
                    if kind == "q" and n == 0:
                        pe.wait_ge(xt_ready, j.count(C, C))
                    w = WQ if kind == "q" else WK
                    terms = [term for c in range(C) for term in (
                        (w_high[:, w, c, tokens], xt_high[:, c]), (w_high[:, w, c, tokens], xt_low[:, c]),
                        (w_low[:, w, c, tokens], xt_high[:, c]))]
                    split_product(full, terms).then_inc(qk_done, 1)
                elif kind == "v":
                    terms = [term for c in range(C) for term in (
                        (xt_high[:, c, tokens], w_high[:, WV, c]), (xt_high[:, c, tokens], w_low[:, WV, c]),
                        (xt_low[:, c, tokens], w_high[:, WV, c]))]
                    split_product(full[:, 0:D], terms).then_inc(v_done, 1)
                else:
                    if n == 0:
                        pe.wait_ge(ctx_ready, j.count(C, C))
                    terms = [term for c in range(C) for term in (
                        (ctx_high[:, j.par, c, tokens], w_high[:, WF, c]),
                        (ctx_high[:, j.par, c, tokens], w_low[:, WF, c]),
                        (ctx_low[:, j.par, c, tokens], w_high[:, WF, c]))]
                    split_product(full[:, 0:D], terms).then_inc(o_done, 1)

            def turn(i):
                peeled = isinstance(i.m, int)
                if not peeled or i.off >= 2:
                    held = {0: ("o", i.plus(-2), 3), 1: ("o", i.plus(-2), 2)}
                elif i.off == 1:
                    held = {0: ("x", Pair(0, 2), 2), 1: ("v", Pair(0, 1), 3)}
                else:
                    held = {0: ("x", Pair(0, 1), 1), 1: ("x", Pair(0, 1), 2)}
                for u in range(UNITS):
                    scores(i, u)
                    if u:
                        turn_probs(i, u - 1)
                    elif not peeled or i.off >= 1:
                        turn_probs(i.plus(-1), UNITS - 1)
                    if u >= 2:
                        times_v(i, u - 2)
                    elif not peeled or i.off >= 1:
                        times_v(i.plus(-1), UNITS - 2 + u)
                    for kind, j, n, bank in work(i, u):
                        pe.wait_ge(*emptied(*held[bank]))
                        make(kind, j, n, bank)
                        held[bank] = (kind, j, n)

            pe.wait_ge(const_ready, 2)
            held = {}
            for kind, j, n, bank in FIRST:
                if bank in held:
                    pe.wait_ge(*emptied(*held[bank]))
                if (kind, n) in (("q", 0), ("k", 0), ("v", 0)):
                    pe.wait_ge(w_ready, "qkv".index(kind) + 1)
                make(kind, Pair(0, j), n, bank)
                held[bank] = (kind, Pair(0, j), n)
            pe.wait_ge(w_ready, 4)
            turns(pe, turn)
            last = Pair(0, PAIRS - 1)
            turn_probs(last, UNITS - 1)
            times_v(last, UNITS - 2)
            times_v(last, UNITS - 1)
            held = {0: ("o", last.plus(-1), 3), 1: ("o", last.plus(-1), 2)}
            for t in range(T):
                pe.wait_ge(*emptied(*held[t % 2]))
                make("o", last, t, t % 2)
                held[t % 2] = ("o", last, t)


_INS = ['x', 'adj', 'L0_gnn_Wq', 'L0_gnn_bq', 'L0_gnn_Wk', 'L0_gnn_bk', 'L0_gnn_Wv', 'L0_gnn_bv', 'L0_gnn_Wf',
        'L0_gnn_bf']


def kernel(**inputs):
    import numpy as _np
    import concourse.bacc as _bacc
    from concourse import mybir as _mybir
    from concourse.bass_utils import run_bass_kernel_spmd as _run

    nc = _bacc.Bacc("TRN2", target_bir_lowering=False, num_devices=1)
    arrays, args = {}, []
    for name in _INS:
        a = _np.ascontiguousarray(inputs[name])
        arrays[f"in_{name}_dram"] = a
        args.append(nc.dram_tensor(f"in_{name}_dram", a.shape, _mybir.dt.from_np(a.dtype), kind="ExternalInput").ap())
    args.append(nc.dram_tensor("out_0_dram", inputs["x"].shape, _mybir.dt.float32, kind="ExternalOutput").ap())
    graph_attention(nc, *args)
    r = _run(nc, [arrays], core_ids=[0])
    return r.results[0]["out_0_dram"]
```

```python
from contextlib import ExitStack

import concourse.bass as bass
from concourse import mybir

F32 = mybir.dt.float32
F32R = mybir.dt.float32r
U8 = mybir.dt.uint8
ALU = mybir.AluOpType
ACT = mybir.ActivationFunctionType

P = 128
NEG = -9000000000000000.0
EPS = 1e-05
SMALLEST_START = 3.0e38


class Pair:

    def __init__(self, m, off):
        self.m, self.off, self.par = m, off, off % 2

    def plus(self, d):
        return Pair(self.m, self.off + d)

    def number(self):
        return self.m * 2 + self.off

    def count(self, per, k):
        return self.m * (2 * per) + (self.off * per + k)

    def dma(self):
        return self.m * 16 + (self.off // 2 * 16 + 16)


def wait(eng, sem, value):
    if not isinstance(value, int) or value > 0:
        eng.wait_ge(sem, value)


def hold(eng, sem, value):
    if not isinstance(value, int):
        eng.wait_ge(sem, value)
        eng.nop(nofuse=True)
    elif value > 0:
        eng.wait_ge(sem, value)


def graph_attention(nc, x, adj, wq, bq, wk, bk, wv, bv, wf, bf, out):
    B, S, D = x.shape
    H = 6
    HD = D // H
    C = D // P
    QT = S // P
    T = 2 * QT
    N = T * P
    PAIRS = B // 2
    UNITS = 2 * C
    TILES = 2 * QT
    SCALE = float(HD) ** -0.5
    assert HD == 64 and QT == 2 and C == 3 and PAIRS % 2 == 0 and PAIRS >= 6

    x_rows = x.rearrange("b s d -> (b s) d").rearrange("(j t p) d -> j p t d", t=T, p=P)
    out_rows = out.rearrange("b s d -> (b s) d").rearrange("(j t p) d -> j p t d", t=T, p=P)
    adj_rows = adj.rearrange("b s k -> (b s) k").rearrange("(j t p) k -> j p t k", t=T, p=P)
    weights = [w.rearrange("(c p) n -> p c n", p=P) for w in (wq, wk, wv, wf)]
    WQ, WK, WV, WF = range(4)

    WORK = [
        [("q", 0, 0), ("k", 0, 1)],
        [("q", 1, 0), ("k", 1, 1), ("v", 0, 0)],
        [("q", 2, 1), ("k", 2, 0)],
        [("v", 1, 1), ("v", 2, 0), ("v", 3, 1)],
        [("x", 0, 0), ("o", 0, 1), ("x", 1, 0), ("o", 1, 1)],
        [("x", 2, 0), ("o", 2, 1), ("o", 3, 0)],
    ]
    FIRST = [("x", 0, 0, 0), ("x", 0, 1, 1), ("x", 0, 2, 0),
             ("q", 0, 0, 1), ("k", 0, 0, 0), ("q", 0, 1, 1), ("k", 0, 1, 0), ("q", 0, 2, 1), ("k", 0, 2, 0),
             ("v", 0, 0, 1), ("v", 0, 1, 0), ("v", 0, 2, 1), ("v", 0, 3, 0),
             ("x", 1, 0, 1), ("x", 1, 1, 0), ("x", 1, 2, 1)]
    AHEAD = {"q": 1, "k": 1, "v": 1, "x": 2, "o": -1}

    def work(i, u):
        for kind, n, bank in WORK[u]:
            j = i.plus(AHEAD[kind])
            if not isinstance(i.m, int) or 0 <= j.off < PAIRS:
                yield kind, j, n, bank

    def turns(eng, turn):
        turn(Pair(0, 0))
        turn(Pair(0, 1))
        with eng.Fori(1, PAIRS // 2 - 1) as m:
            turn(Pair(m, 0))
            turn(Pair(m, 1))
        turn(Pair(0, PAIRS - 2))
        turn(Pair(0, PAIRS - 1))

    with ExitStack() as ctx:
        def sb(name, shape, dt):
            return ctx.enter_context(nc.sbuf_tensor(name, shape, dt))

        def psum(name):
            return ctx.enter_context(nc.psum_tensor(name, [P, 512], F32))

        def sem(name):
            return ctx.enter_context(nc.semaphore(name))

        ident = sb("ident", [P, P], F32)
        neg_half = sb("neg_half", [P, T], F32)
        bq_col = sb("bq_col", [P, C], F32)
        bk_col = sb("bk_col", [P, C], F32)
        bv_col = sb("bv_col", [P, C], F32)
        bf_row = sb("bf_row", [P, D], F32)
        w_high = sb("w_high", [P, 4, C, D], F32R)
        w_low = sb("w_low", [P, 4, C, D], F32R)
        x_raw = sb("x_raw", [P, 2, T, D], F32)
        xt_high = sb("xt_high", [P, C, N], F32R)
        xt_low = sb("xt_low", [P, C, N], F32R)
        k_high = sb("k_high", [P, 2, C, N], F32R)
        q_stack = sb("q_stack", [P, 2, C, 2, N], F32R)
        k_stack = sb("k_stack", [P, 2, C, 2, N], F32R)
        v_sb = sb("v_sb", [P, 2, T, D], F32)
        adj_raw = sb("adj_raw", [P, 2, T, S], U8)
        mask = sb("mask", [P, 2, T, S], F32)
        probs = sb("probs", [P, 2, TILES, S], F32)
        low_col = sb("low_col", [P, UNITS * TILES], F32)
        sum_col = sb("sum_col", [P, UNITS * TILES], F32)
        inv_col = sb("inv_col", [P, UNITS * TILES], F32)
        probs_t = sb("probs_t", [P, 2, 2, 512], F32)
        ctx_high = sb("ctx_high", [P, 2, C, N], F32R)
        ctx_low = sb("ctx_low", [P, 2, C, N], F32R)
        resid = sb("resid", [P, T, D], F32)
        y_sb = sb("y_sb", [P, 2, T, D], F32)
        stats = sb("stats", [P, T, 6], F32)
        mean_var = sb("mean_var", [P, T, 2], F32)
        var_eps = sb("var_eps", [P, T], F32)
        rstd = sb("rstd", [P, T], F32)

        w_raw = [y_sb[:, 0, 0:C], y_sb[:, 1, 0:C], resid[:, 0:C],
                 probs_t[:].rearrange("p a h n -> p (a h n)")[:, 0:C * D].rearrange("p (c n) -> p c n", c=C)]

        score_bank = [psum(f"score_bank{n}") for n in range(3)]
        turned_bank = [psum(f"turned_bank{n}") for n in range(2)]
        ctx_bank = psum("ctx_bank")
        proj_bank = [psum(f"proj_bank{n}") for n in range(2)]

        x_loaded = [sem(f"x_loaded{n}") for n in range(2)]
        adj_loaded = [sem(f"adj_loaded{n}") for n in range(2)]
        w_loaded = [sem(f"w_loaded{n}") for n in range(4)]
        bias_loaded = sem("bias_loaded")
        resid_loaded = sem("resid_loaded")
        out_stored = [sem(f"out_stored{n}") for n in range(2)]
        ident_zero = sem("ident_zero")
        const_ready = sem("const_ready")
        w_high_ready = sem("w_high_ready")
        w_ready = sem("w_ready")
        x_turned = sem("x_turned")
        xt_high_ready = sem("xt_high_ready")
        xt_ready = sem("xt_ready")
        qk_done = sem("qk_done")
        qk_high_ready = sem("qk_high_ready")
        qk_ready = sem("qk_ready")
        k_shifted = sem("k_shifted")
        v_done = sem("v_done")
        v_ready = sem("v_ready")
        o_done = sem("o_done")
        y_ready = sem("y_ready")
        mask_built = sem("mask_built")
        scores_done = sem("scores_done")
        masked = sem("masked")
        exp_done = sem("exp_done")
        inv_ready = sem("inv_ready")
        scaled = sem("scaled")
        p_turned = sem("p_turned")
        pt_ready = sem("pt_ready")
        pv_done = sem("pv_done")
        ctx_high_ready = sem("ctx_high_ready")
        ctx_ready = sem("ctx_ready")
        resid_ready = sem("resid_ready")
        stats_ready = sem("stats_ready")
        var_ready = sem("var_ready")
        eps_added = sem("eps_added")
        rstd_ready = sem("rstd_ready")
        normed = sem("normed")

        def emptied(kind, j, n):
            return {"x": (xt_ready, j.count(C, n + 1)), "q": (qk_ready, j.count(4 * C, 4 * n + 2)),
                    "k": (qk_ready, j.count(4 * C, 4 * n + 4)), "v": (v_ready, j.count(T, n + 1)),
                    "o": (y_ready, j.count(T, n + 1))}[kind]

        halves = [slice(h * HD, (h + 1) * HD) for h in range(2)]

        block = ctx.enter_context(nc.Block())

        @block.sync
        def _(sp):
            def load_x(j):
                hold(sp, x_turned, j.plus(-2).count(C, C))
                sp.dma_start(x_raw[:, j.par], x_rows[j.number()]).then_inc(x_loaded[j.par], 16)

            def load_adj(j):
                hold(sp, mask_built, j.plus(-2).count(2, 2))
                sp.dma_start(adj_raw[:, j.par], adj_rows[j.number()]).then_inc(adj_loaded[j.par], 16)

            def load_resid(j):
                hold(sp, y_ready, j.plus(-1).count(T, T))
                sp.dma_start(resid[:], x_rows[j.number()]).then_inc(resid_loaded, 16)

            def store(j):
                hold(sp, normed, j.count(T, T))
                sp.dma_start(out_rows[j.number()], y_sb[:, j.par]).then_inc(out_stored[j.par], 16)

            def turn(i):
                peeled = isinstance(i.m, int)
                if not peeled or i.off + 2 < PAIRS:
                    load_x(i.plus(2))
                if not peeled or i.off + 1 < PAIRS:
                    load_adj(i.plus(1))
                if not peeled or i.off >= 1:
                    load_resid(i.plus(-1))
                if not peeled or i.off >= 2:
                    store(i.plus(-2))

            load_x(Pair(0, 0))
            for n in (WQ, WK):
                sp.dma_start(w_raw[n], weights[n]).then_inc(w_loaded[n], 16)
            for column, bias in ((bq_col, bq), (bk_col, bk), (bv_col, bv)):
                sp.dma_start(column[:], bias.rearrange("(c p) -> p c", p=P),
                             allow_slow_non_contiguous=True).then_inc(bias_loaded, 16)
            sp.dma_start(bf_row[:], bf.partition_broadcast(P)).then_inc(bias_loaded, 16)
            load_adj(Pair(0, 0))
            for n in (WV, WF):
                sp.dma_start(w_raw[n], weights[n]).then_inc(w_loaded[n], 16)
            load_x(Pair(0, 1))
            sp.wait_ge(w_ready, 4)
            turns(sp, turn)
            load_resid(Pair(0, PAIRS - 1))
            store(Pair(0, PAIRS - 2))
            store(Pair(0, PAIRS - 1))
            for par in range(2):
                sp.wait_ge(out_stored[par], 16 * (PAIRS // 2))

        @block.gpsimd
        def _(pool):
            def build_mask(j, g):
                hold(pool, masked, j.plus(-2).count(UNITS * TILES, UNITS * TILES))
                if g == 0:
                    hold(pool, adj_loaded[j.par], j.dma())
                rows = slice(g * QT, (g + 1) * QT)
                nc.gpsimd.tensor_scalar(mask[:, j.par, rows], adj_raw[:, j.par, rows], -NEG / SCALE, NEG / SCALE,
                                        ALU.mult, ALU.add).then_inc(mask_built, 1)

            def scale_probs(i, u):
                hold(pool, inv_ready, i.count(UNITS, u + 1))
                for k in range(TILES):
                    tile = probs[:, u % 2, k]
                    at = u * TILES + k
                    nc.gpsimd.tensor_scalar(tile, tile, inv_col[:, at:at + 1], 1.0, ALU.mult,
                                            ALU.mult).then_inc(scaled, 1)

            def add_bias(j, t):
                if t == 0:
                    pool.wait_ge(resid_loaded, j.m * 32 + (j.off * 16 + 16))
                nc.gpsimd.tensor_tensor(resid[:, t], resid[:, t], bf_row[:], ALU.add).then_inc(resid_ready, 1)

            def make_rstd(j):
                hold(pool, var_ready, j.count(T, T))
                nc.gpsimd.tensor_scalar(var_eps[:], mean_var[:, :, 1], EPS, None, ALU.add).then_inc(eps_added, 1)
                hold(pool, eps_added, j.count(1, 1))
                nc.gpsimd.tensor_tensor(rstd[:], var_eps[:], neg_half[:], ALU.pow).then_inc(rstd_ready, 1)

            def turn(i):
                peeled = isinstance(i.m, int)
                for u in range(UNITS):
                    if u == 4 and (not peeled or i.off >= 2):
                        make_rstd(i.plus(-2))
                    scale_probs(i, u)
                    if u < 2 and (not peeled or i.off + 1 < PAIRS):
                        build_mask(i.plus(1), u)
                    if u in (2, 3) and (not peeled or i.off >= 1):
                        add_bias(i.plus(-1), 2 * u - 4)
                        add_bias(i.plus(-1), 2 * u - 3)

            nc.gpsimd.memset(ident[:], 0.0).then_inc(ident_zero, 1)
            nc.gpsimd.memset(neg_half[:], -0.5).then_inc(const_ready, 1)
            pool.wait_ge(ident_zero, 1)
            nc.gpsimd.affine_select(out=ident[:], in_=ident[:], compare_op=ALU.not_equal, fill=1.0, base=0,
                                    pattern=[[-1, P]], channel_multiplier=1).then_inc(const_ready, 1)
            pool.wait_ge(const_ready, 2)
            for g in range(2):
                build_mask(Pair(0, 0), g)
            pool.wait_ge(bias_loaded, 64)
            turns(pool, turn)
            make_rstd(Pair(0, PAIRS - 2))
            for t in range(T):
                add_bias(Pair(0, PAIRS - 1), t)
            make_rstd(Pair(0, PAIRS - 1))

        @block.scalar
        def _(act):
            def split_weight(n):
                act.wait_ge(w_loaded[n], 16)
                nc.scalar.copy(w_high[:, n], w_raw[n]).then_inc(w_high_ready, 1)

            def exps(i, u):
                for k in range(TILES):
                    at = u * TILES + k
                    act.wait_ge(masked, i.count(UNITS * TILES, at + 1))
                    tile = probs[:, u % 2, k]
                    nc.scalar.activation(tile, tile, ACT.Exp, bias=low_col[:, at:at + 1], scale=-1.0,
                                         accum_out=sum_col[:, at:at + 1]).then_inc(exp_done, 1)

            def copy_turned(i, u):
                wait(act, pv_done, i.count(UNITS, u - 1))
                for h in range(2):
                    act.wait_ge(p_turned, i.count(2 * UNITS, 2 * u + h + 1))
                    nc.scalar.copy(probs_t[:, u % 2, h], turned_bank[h][:]).then_inc(pt_ready, 1)

            def context_high(i, c):
                act.wait_ge(pv_done, i.count(UNITS, 2 * c + 2))
                nc.scalar.activation(ctx_high[:, i.par, c], ctx_bank[:], ACT.Identity,
                                     bias=bv_col[:, c:c + 1]).then_inc(ctx_high_ready, 1)

            def take(kind, j, n, bank):
                if kind == "x":
                    act.wait_ge(x_turned, j.count(C, n + 1))
                    nc.scalar.copy(xt_high[:, n], proj_bank[bank][:]).then_inc(xt_high_ready, 1)
                elif kind == "q":
                    act.wait_ge(qk_done, j.count(2 * C, 2 * n + 1))
                    for h in range(2):
                        d = halves[h]
                        nc.scalar.activation(q_stack[d, j.par, n, h], proj_bank[bank][d, :], ACT.Identity,
                                             bias=bq_col[d, n:n + 1]).then_inc(qk_high_ready, 1)
                elif kind == "k":
                    act.wait_ge(qk_done, j.count(2 * C, 2 * n + 2))
                    nc.scalar.activation(k_high[:, j.par, n], proj_bank[bank][:], ACT.Identity,
                                         bias=bk_col[:, n:n + 1]).then_inc(qk_high_ready, 1)
                elif kind == "v":
                    act.wait_ge(v_done, j.count(T, n + 1))
                    nc.scalar.copy(v_sb[:, j.par, n], proj_bank[bank][:, 0:D]).then_inc(v_ready, 1)

            def turn(i):
                follows = not isinstance(i.m, int) or i.off >= 1
                for u in range(UNITS):
                    pieces = list(work(i, u))
                    exps(i, u)
                    for piece in pieces[:1]:
                        take(*piece)
                    if u:
                        copy_turned(i, u - 1)
                    elif follows:
                        copy_turned(i.plus(-1), UNITS - 1)
                    for piece in pieces[1:2]:
                        take(*piece)
                    if u in (3, 5):
                        context_high(i, u // 2 - 1)
                    if u == 1 and follows:
                        context_high(i.plus(-1), C - 1)
                    for piece in pieces[2:]:
                        take(*piece)

            split_weight(WQ)
            for kind, j, n, bank in FIRST[:3]:
                take(kind, Pair(0, j), n, bank)
            split_weight(WK)
            act.wait_ge(bias_loaded, 64)
            for kind, j, n, bank in FIRST[3:9]:
                take(kind, Pair(0, j), n, bank)
            split_weight(WV)
            for kind, j, n, bank in FIRST[9:]:
                take(kind, Pair(0, j), n, bank)
            split_weight(WF)
            turns(act, turn)
            copy_turned(Pair(0, PAIRS - 1), UNITS - 1)
            context_high(Pair(0, PAIRS - 1), C - 1)

        @block.vector
        def _(dve):
            def split_weight(n):
                dve.wait_ge(w_high_ready, n + 1)
                nc.vector.tensor_tensor(w_low[:, n], w_raw[n], w_high[:, n].bitcast(F32),
                                        ALU.subtract).then_inc(w_ready, 1)

            def mask_scores(i, u):
                if u == 0:
                    hold(dve, mask_built, i.count(2, 2))
                hold(dve, p_turned, i.count(2 * UNITS, 2 * (u - 1)))
                for k in range(TILES):
                    h, q = k // QT, k % QT
                    at = u * TILES + k
                    if q == 0:
                        hold(dve, scores_done, i.count(2 * UNITS, 2 * u + h + 1))
                    nc.vector.tensor_tensor_reduce(
                        out=probs[:, u % 2, k], in0=score_bank[(2 * u + h) % 3][:, q * S:(q + 1) * S],
                        in1=mask[:, i.par, (u % 2) * QT + q], scale=-SCALE, scalar=SMALLEST_START, op0=ALU.add,
                        op1=ALU.min, accum_out=low_col[:, at:at + 1]).then_inc(masked, 1)

            def invert_sums(i, u):
                dve.wait_ge(exp_done, i.count(UNITS * TILES, (u + 1) * TILES))
                cols = slice(u * TILES, (u + 1) * TILES)
                nc.vector.reciprocal(inv_col[:, cols], sum_col[:, cols]).then_inc(inv_ready, 1)

            def context_low(i, c):
                dve.wait_ge(ctx_high_ready, i.count(C, c + 1))
                nc.vector.scalar_tensor_tensor(out=ctx_low[:, i.par, c], in0=ctx_bank[:], scalar=bv_col[:, c:c + 1],
                                               in1=ctx_high[:, i.par, c].bitcast(F32), op0=ALU.add,
                                               op1=ALU.subtract).then_inc(ctx_ready, 1)

            def take(kind, j, n, bank):
                if kind == "x":
                    dve.wait_ge(xt_high_ready, j.count(C, n + 1))
                    nc.vector.tensor_tensor(xt_low[:, n], proj_bank[bank][:], xt_high[:, n].bitcast(F32),
                                            ALU.subtract).then_inc(xt_ready, 1)
                elif kind == "q":
                    for h in range(2):
                        d, other = halves[h], halves[1 - h]
                        dve.wait_ge(qk_high_ready, j.count(3 * C, 3 * n + h + 1))
                        nc.vector.scalar_tensor_tensor(
                            out=q_stack[other, j.par, n, h], in0=proj_bank[bank][d, :], scalar=bq_col[d, n:n + 1],
                            in1=q_stack[d, j.par, n, h].bitcast(F32), op0=ALU.add,
                            op1=ALU.subtract).then_inc(qk_ready, 1)
                elif kind == "k":
                    dve.wait_ge(qk_high_ready, j.count(3 * C, 3 * n + 3))
                    for h in range(2):
                        d = halves[h]
                        nc.vector.scalar_tensor_tensor(
                            out=k_stack[d, j.par, n, h], in0=proj_bank[bank][d, :], scalar=bk_col[d, n:n + 1],
                            in1=k_high[d, j.par, n].bitcast(F32), op0=ALU.add,
                            op1=ALU.subtract).then_inc(qk_ready, 1)
                elif kind == "o":
                    if n == 0:
                        wait(dve, out_stored[j.par], j.plus(-2).dma())
                    dve.wait_ge(resid_ready, j.count(T, n + 1))
                    dve.wait_ge(o_done, j.count(T, n + 1))
                    nc.vector.tensor_tensor(y_sb[:, j.par, n], proj_bank[bank][:, 0:D], resid[:, n],
                                            ALU.add).then_inc(y_ready, 1)

            def shift_k(j, n):
                for h in range(2):
                    d, other = halves[h], halves[1 - h]
                    nc.vector.tensor_copy(k_stack[other, j.par, n, h],
                                          k_high[d, j.par, n].bitcast(F32)).then_inc(k_shifted, 1)

            def moments(j):
                dve.wait_ge(y_ready, j.count(T, T))
                for t in range(T):
                    nc.vector.bn_stats(stats[:, t], y_sb[:, j.par, t]).then_inc(stats_ready, 1)
                for t in range(T):
                    hold(dve, stats_ready, j.count(T, t + 1))
                    nc.vector.bn_aggr(mean_var[:, t], stats[:, t]).then_inc(var_ready, 1)

            def normalise(j):
                dve.wait_ge(rstd_ready, j.count(1, 1))
                for t in range(T):
                    nc.vector.tensor_scalar(y_sb[:, j.par, t], y_sb[:, j.par, t], mean_var[:, t, 0:1],
                                            rstd[:, t:t + 1], ALU.subtract, ALU.mult).then_inc(normed, 1)

            def turn(i):
                peeled = isinstance(i.m, int)
                for u in range(UNITS):
                    pieces = list(work(i, u))
                    mask_scores(i, u)
                    if 1 <= u <= C and (not peeled or i.off + 1 < PAIRS):
                        shift_k(i.plus(1), u - 1)
                    if u == 5 and (not peeled or i.off >= 2):
                        normalise(i.plus(-2))
                    invert_sums(i, u)
                    if u == 3 and (not peeled or i.off >= 2):
                        moments(i.plus(-2))
                    for piece in pieces[:2]:
                        take(*piece)
                    if u in (3, 5):
                        context_low(i, u // 2 - 1)
                    if u == 1 and (not peeled or i.off >= 1):
                        context_low(i.plus(-1), C - 1)
                    for piece in pieces[2:]:
                        take(*piece)

            split_weight(WQ)
            for kind, j, n, bank in FIRST[:3]:
                take(kind, Pair(0, j), n, bank)
            split_weight(WK)
            for kind, j, n, bank in FIRST[3:9]:
                take(kind, Pair(0, j), n, bank)
                if kind == "k":
                    shift_k(Pair(0, j), n)
            split_weight(WV)
            for kind, j, n, bank in FIRST[9:]:
                take(kind, Pair(0, j), n, bank)
            split_weight(WF)
            turns(dve, turn)
            last = Pair(0, PAIRS - 1)
            moments(last.plus(-1))
            context_low(last, C - 1)
            normalise(last.plus(-1))
            for t in range(T):
                take("o", last, t, t % 2)
            moments(last)
            normalise(last)

        @block.tensor
        def _(pe):
            def split_product(bank_ap, terms):
                for n, (stationary, moving) in enumerate(terms):
                    last = nc.tensor.matmul(bank_ap, stationary, moving, start=(n == 0), stop=(n == len(terms) - 1))
                return last

            def scores(i, u):
                c, g = u // 2, u % 2
                banks = [score_bank[(2 * u + h) % 3] for h in range(2)]
                if g == 0:
                    pe.wait_ge(qk_ready, i.count(4 * C, 4 * c + 4))
                    pe.wait_ge(k_shifted, i.count(2 * C, 2 * c + 2))
                wait(pe, masked, i.count(UNITS * TILES, 2 * (2 * u + 1) - 4))
                keys = slice(g * S, (g + 1) * S)
                for q in range(QT):
                    rows = slice(g * S + q * P, g * S + (q + 1) * P)
                    for h in range(2):
                        nc.tensor.matmul(banks[h][:, q * S:(q + 1) * S], q_stack[:, i.par, c, h, rows],
                                         k_stack[:, i.par, c, h, keys], start=True, stop=False)
                    for h in range(2):
                        d = halves[h]
                        mm = nc.tensor.matmul(banks[h][:, q * S:(q + 1) * S], q_stack[d, i.par, c, h, rows],
                                              k_high[d, i.par, c, keys], start=False, stop=True)
                        if q == QT - 1:
                            mm.then_inc(scores_done, 1)

            def turn_probs(i, u):
                for h in range(2):
                    pe.wait_ge(scaled, i.count(UNITS * TILES, u * TILES + (h + 1) * QT))
                    wait(pe, pt_ready, i.count(2 * UNITS, 2 * (u - 1) + h + 1))
                    for q in range(QT):
                        for k in range(QT):
                            at = k * S + q * P
                            mm = nc.tensor.transpose(turned_bank[h][:, at:at + P],
                                                     probs[:, u % 2, h * QT + q, k * P:(k + 1) * P], ident[:])
                    mm.then_inc(p_turned, 1)

            def times_v(i, u):
                c, g = u // 2, u % 2
                if u == 0:
                    pe.wait_ge(v_ready, i.count(T, T))
                if g == 0:
                    wait(pe, ctx_ready, i.count(C, c))
                pe.wait_ge(pt_ready, i.count(2 * UNITS, 2 * u + 2))
                for k in range(QT):
                    for h in range(2):
                        d = halves[h]
                        feats = slice(c * P + h * HD, c * P + (h + 1) * HD)
                        mm = nc.tensor.matmul(ctx_bank[d, g * S:(g + 1) * S], v_sb[:, i.par, g * QT + k, feats],
                                              probs_t[:, u % 2, h, k * S:(k + 1) * S],
                                              start=(k == 0), stop=(k == QT - 1))
                mm.then_inc(pv_done, 1)

            def make(kind, j, n, bank):
                full = proj_bank[bank][:]
                tokens = slice(n * P, (n + 1) * P)
                if kind == "x":
                    if n == 0:
                        pe.wait_ge(x_loaded[j.par], j.dma())
                    for t in range(T):
                        mm = nc.tensor.transpose(full[:, t * P:(t + 1) * P], x_raw[:, j.par, t, tokens], ident[:])
                    mm.then_inc(x_turned, 1)
                elif kind in "qk":
                    if kind == "q" and n == 0:
                        pe.wait_ge(xt_ready, j.count(C, C))
                    w = WQ if kind == "q" else WK
                    terms = [term for c in range(C) for term in (
                        (w_high[:, w, c, tokens], xt_high[:, c]), (w_high[:, w, c, tokens], xt_low[:, c]),
                        (w_low[:, w, c, tokens], xt_high[:, c]))]
                    split_product(full, terms).then_inc(qk_done, 1)
                elif kind == "v":
                    terms = [term for c in range(C) for term in (
                        (xt_high[:, c, tokens], w_high[:, WV, c]), (xt_high[:, c, tokens], w_low[:, WV, c]),
                        (xt_low[:, c, tokens], w_high[:, WV, c]))]
                    split_product(full[:, 0:D], terms).then_inc(v_done, 1)
                else:
                    if n == 0:
                        pe.wait_ge(ctx_ready, j.count(C, C))
                    terms = [term for c in range(C) for term in (
                        (ctx_high[:, j.par, c, tokens], w_high[:, WF, c]),
                        (ctx_high[:, j.par, c, tokens], w_low[:, WF, c]),
                        (ctx_low[:, j.par, c, tokens], w_high[:, WF, c]))]
                    split_product(full[:, 0:D], terms).then_inc(o_done, 1)

            def turn(i):
                peeled = isinstance(i.m, int)
                if not peeled or i.off >= 2:
                    held = {0: ("o", i.plus(-2), 3), 1: ("o", i.plus(-2), 2)}
                elif i.off == 1:
                    held = {0: ("x", Pair(0, 2), 2), 1: ("v", Pair(0, 1), 3)}
                else:
                    held = {0: ("x", Pair(0, 1), 1), 1: ("x", Pair(0, 1), 2)}

                def make_next(pieces):
                    for kind, j, n, bank in pieces:
                        pe.wait_ge(*emptied(*held[bank]))
                        make(kind, j, n, bank)
                        held[bank] = (kind, j, n)

                if peeled and i.off == 1:
                    pe.wait_ge(w_ready, 4)
                for u in range(UNITS):
                    pieces = list(work(i, u))
                    scores(i, u)
                    make_next(pieces[:1])
                    if u:
                        turn_probs(i, u - 1)
                    elif not peeled or i.off >= 1:
                        turn_probs(i.plus(-1), UNITS - 1)
                    make_next(pieces[1:2])
                    if u >= 2:
                        times_v(i, u - 2)
                    elif not peeled or i.off >= 1:
                        times_v(i.plus(-1), UNITS - 2 + u)
                    make_next(pieces[2:])

            pe.wait_ge(const_ready, 2)
            held = {}
            for kind, j, n, bank in FIRST:
                if bank in held:
                    pe.wait_ge(*emptied(*held[bank]))
                if (kind, n) in (("q", 0), ("k", 0), ("v", 0)):
                    pe.wait_ge(w_ready, "qkv".index(kind) + 1)
                make(kind, Pair(0, j), n, bank)
                held[bank] = (kind, Pair(0, j), n)
            turns(pe, turn)
            last = Pair(0, PAIRS - 1)
            turn_probs(last, UNITS - 1)
            times_v(last, UNITS - 2)
            times_v(last, UNITS - 1)
            held = {0: ("o", last.plus(-1), 3), 1: ("o", last.plus(-1), 2)}
            for t in range(T):
                pe.wait_ge(*emptied(*held[t % 2]))
                make("o", last, t, t % 2)
                held[t % 2] = ("o", last, t)


_INS = ['x', 'adj', 'L0_gnn_Wq', 'L0_gnn_bq', 'L0_gnn_Wk', 'L0_gnn_bk', 'L0_gnn_Wv', 'L0_gnn_bv', 'L0_gnn_Wf',
        'L0_gnn_bf']


def kernel(**inputs):
    import numpy as _np
    import concourse.bacc as _bacc
    from concourse import mybir as _mybir
    from concourse.bass_utils import run_bass_kernel_spmd as _run

    nc = _bacc.Bacc("TRN2", target_bir_lowering=False, num_devices=1)
    arrays, args = {}, []
    for name in _INS:
        a = _np.ascontiguousarray(inputs[name])
        arrays[f"in_{name}_dram"] = a
        args.append(nc.dram_tensor(f"in_{name}_dram", a.shape, _mybir.dt.from_np(a.dtype), kind="ExternalInput").ap())
    args.append(nc.dram_tensor("out_0_dram", inputs["x"].shape, _mybir.dt.float32, kind="ExternalOutput").ap())
    graph_attention(nc, *args)
    r = _run(nc, [arrays], core_ids=[0])
    return r.results[0]["out_0_dram"]
```

```python
from contextlib import ExitStack

import concourse.bass as bass
from concourse import mybir

F32 = mybir.dt.float32
F32R = mybir.dt.float32r
U8 = mybir.dt.uint8
ALU = mybir.AluOpType
ACT = mybir.ActivationFunctionType

P = 128
NEG = -9000000000000000.0
EPS = 1e-05
SMALLEST_START = 3.0e38


class Pair:

    def __init__(self, m, off):
        self.m, self.off, self.par = m, off, off % 2

    def plus(self, d):
        return Pair(self.m, self.off + d)

    def number(self):
        return self.m * 2 + self.off

    def count(self, per, k):
        return self.m * (2 * per) + (self.off * per + k)

    def dma(self):
        return self.m * 16 + (self.off // 2 * 16 + 16)


def wait(eng, sem, value):
    if not isinstance(value, int) or value > 0:
        eng.wait_ge(sem, value)


def hold(eng, sem, value):
    if not isinstance(value, int):
        eng.wait_ge(sem, value)
        eng.nop(nofuse=True)
    elif value > 0:
        eng.wait_ge(sem, value)


def graph_attention(nc, x, adj, wq, bq, wk, bk, wv, bv, wf, bf, out):
    B, S, D = x.shape
    H = 6
    HD = D // H
    C = D // P
    QT = S // P
    T = 2 * QT
    N = T * P
    PAIRS = B // 2
    UNITS = 2 * C
    TILES = 2 * QT
    SCALE = float(HD) ** -0.5
    assert HD == 64 and QT == 2 and C == 3 and PAIRS % 2 == 0 and PAIRS >= 6

    x_rows = x.rearrange("b s d -> (b s) d").rearrange("(j t p) d -> j p t d", t=T, p=P)
    out_rows = out.rearrange("b s d -> (b s) d").rearrange("(j t p) d -> j p t d", t=T, p=P)
    adj_rows = adj.rearrange("b s k -> (b s) k").rearrange("(j t p) k -> j p t k", t=T, p=P)
    weights = [w.rearrange("(c p) n -> p c n", p=P) for w in (wq, wk, wv, wf)]
    WQ, WK, WV, WF = range(4)

    WORK = [
        [("q", 0, 0), ("k", 0, 1)],
        [("q", 1, 0), ("k", 1, 1), ("v", 0, 0)],
        [("q", 2, 1), ("k", 2, 0)],
        [("v", 1, 1), ("v", 2, 0), ("v", 3, 1)],
        [("x", 0, 0), ("o", 0, 1), ("x", 1, 0), ("o", 1, 1)],
        [("x", 2, 0), ("o", 2, 1), ("o", 3, 0)],
    ]
    FIRST = [("x", 0, 0, 5), ("x", 0, 1, 6), ("x", 0, 2, 7),
             ("q", 0, 0, 0), ("k", 0, 0, 1), ("q", 0, 1, 2), ("k", 0, 1, 3), ("q", 0, 2, 4), ("k", 0, 2, 0),
             ("v", 0, 0, 1), ("v", 0, 1, 2), ("v", 0, 2, 0), ("v", 0, 3, 2),
             ("x", 1, 0, 1), ("x", 1, 1, 0), ("x", 1, 2, 1)]
    LAST_BANKS = (0, 5, 6, 7)
    WORK_FIRST = WORK[:4] + [[("x", 0, 0), ("x", 1, 1)], [("x", 2, 0)]]
    WORK_BEFORE_LAST = [[("q", 0, 0), ("k", 0, 1)], [("q", 1, 0), ("k", 1, 1)], [("q", 2, 0), ("k", 2, 1)],
                        [("o", 0, 0), ("o", 1, 1)], [("o", 2, 0), ("v", 0, 1)], [("o", 3, 0)]]
    WORK_LAST = [[("v", 1, 1), ("v", 2, 0)], [("v", 3, 1)], [("o", 0, 0)], [("o", 1, 1)], [("o", 2, 0)], [("o", 3, 1)]]
    AHEAD = {"q": 1, "k": 1, "v": 1, "x": 2, "o": -1}

    def work(i, u):
        table = WORK
        if isinstance(i.m, int):
            table = {0: WORK_FIRST, PAIRS - 2: WORK_BEFORE_LAST, PAIRS - 1: WORK_LAST}.get(i.off, WORK)
        for kind, n, bank in table[u]:
            j = i.plus(0 if table is WORK_LAST and kind == "v" else AHEAD[kind])
            if not isinstance(i.m, int) or 0 <= j.off < PAIRS:
                yield kind, j, n, bank

    def turns(eng, turn):
        turn(Pair(0, 0))
        turn(Pair(0, 1))
        with eng.Fori(1, PAIRS // 2 - 1) as m:
            turn(Pair(m, 0))
            turn(Pair(m, 1))
        turn(Pair(0, PAIRS - 2))
        turn(Pair(0, PAIRS - 1))

    with ExitStack() as ctx:
        def sb(name, shape, dt):
            return ctx.enter_context(nc.sbuf_tensor(name, shape, dt))

        def psum(name):
            return ctx.enter_context(nc.psum_tensor(name, [P, 512], F32))

        def sem(name):
            return ctx.enter_context(nc.semaphore(name))

        ident = sb("ident", [P, P], F32)
        neg_half = sb("neg_half", [P, T], F32)
        bq_col = sb("bq_col", [P, C], F32)
        bk_col = sb("bk_col", [P, C], F32)
        bv_col = sb("bv_col", [P, C], F32)
        bf_row = sb("bf_row", [P, D], F32)
        w_high = sb("w_high", [P, 4, C, D], F32R)
        w_low = sb("w_low", [P, 4, C, D], F32R)
        x_raw = sb("x_raw", [P, 2, T, D], F32)
        xt_high = sb("xt_high", [P, C, N], F32R)
        xt_low = sb("xt_low", [P, C, N], F32R)
        k_high = sb("k_high", [P, 2, C, N], F32R)
        q_stack = sb("q_stack", [P, 2, C, 2, N], F32R)
        k_stack = sb("k_stack", [P, 2, C, 2, N], F32R)
        v_sb = sb("v_sb", [P, 2, T, D], F32)
        adj_raw = sb("adj_raw", [P, 2, T, S], U8)
        mask = sb("mask", [P, 2, T, S], F32)
        probs = sb("probs", [P, 2, TILES, S], F32)
        low_col = sb("low_col", [P, UNITS * TILES], F32)
        sum_col = sb("sum_col", [P, UNITS * TILES], F32)
        inv_col = sb("inv_col", [P, UNITS * TILES], F32)
        probs_t = sb("probs_t", [P, 2, 2, 512], F32)
        ctx_high = sb("ctx_high", [P, 2, C, N], F32R)
        ctx_low = sb("ctx_low", [P, 2, C, N], F32R)
        resid = sb("resid", [P, T, D], F32)
        y_sb = sb("y_sb", [P, 2, T, D], F32)
        stats = sb("stats", [P, T, 6], F32)
        mean_var = sb("mean_var", [P, T, 2], F32)
        var_eps = sb("var_eps", [P, T], F32)
        rstd = sb("rstd", [P, T], F32)

        w_raw = [y_sb[:, 0, 0:C], y_sb[:, 1, 0:C], resid[:, 0:C],
                 v_sb[:, 1, 1:1 + C]]

        score_bank = [psum(f"score_bank{n}") for n in range(3)]
        turned_bank = [psum(f"turned_bank{n}") for n in range(2)]
        ctx_bank = psum("ctx_bank")
        proj_bank = [psum(f"proj_bank{n}") for n in range(2)] + [ctx_bank] + turned_bank + score_bank

        x_loaded = [sem(f"x_loaded{n}") for n in range(2)]
        adj_loaded = [sem(f"adj_loaded{n}") for n in range(2)]
        w_loaded = [sem(f"w_loaded{n}") for n in range(4)]
        bias_loaded = sem("bias_loaded")
        resid_loaded = sem("resid_loaded")
        out_stored = [sem(f"out_stored{n}") for n in range(2)]
        last_stored = sem("last_stored")
        ident_zero = sem("ident_zero")
        const_ready = sem("const_ready")
        w_high_ready = sem("w_high_ready")
        w_ready = [sem(f"w_ready{n}") for n in range(4)]
        x_turned = sem("x_turned")
        xt_high_ready = sem("xt_high_ready")
        xt_ready = sem("xt_ready")
        qk_done = sem("qk_done")
        qk_high_ready = sem("qk_high_ready")
        qk_ready = sem("qk_ready")
        k_shifted = sem("k_shifted")
        v_done = sem("v_done")
        v_ready = sem("v_ready")
        o_done = sem("o_done")
        y_ready = sem("y_ready")
        mask_built = sem("mask_built")
        scores_done = sem("scores_done")
        masked = sem("masked")
        exp_done = sem("exp_done")
        inv_ready = sem("inv_ready")
        scaled = sem("scaled")
        p_turned = sem("p_turned")
        pt_ready = sem("pt_ready")
        pv_done = sem("pv_done")
        ctx_high_ready = sem("ctx_high_ready")
        ctx_ready = sem("ctx_ready")
        resid_ready = sem("resid_ready")
        stats_ready = sem("stats_ready")
        var_ready = sem("var_ready")
        eps_added = sem("eps_added")
        rstd_ready = sem("rstd_ready")
        normed = sem("normed")

        def emptied(kind, j, n):
            return {"x": (xt_ready, j.count(C, n + 1)), "q": (qk_ready, j.count(4 * C, 4 * n + 2)),
                    "k": (qk_ready, j.count(4 * C, 4 * n + 4)), "v": (v_ready, j.count(T, n + 1)),
                    "o": (y_ready, j.count(T, n + 1))}[kind]

        halves = [slice(h * HD, (h + 1) * HD) for h in range(2)]

        last_ctx_bank = [ctx_bank, proj_bank[1]]

        block = ctx.enter_context(nc.Block())

        @block.sync
        def _(sp):
            def load_x(j):
                hold(sp, x_turned, j.plus(-2).count(C, C))
                sp.dma_start(x_raw[:, j.par], x_rows[j.number()]).then_inc(x_loaded[j.par], 16)

            def load_adj(j):
                hold(sp, mask_built, j.plus(-2).count(2, 2))
                sp.dma_start(adj_raw[:, j.par], adj_rows[j.number()]).then_inc(adj_loaded[j.par], 16)

            def load_resid(j):
                hold(sp, y_ready, j.plus(-1).count(T, T))
                sp.dma_start(resid[:], x_rows[j.number()]).then_inc(resid_loaded, 16)

            def store(j):
                hold(sp, normed, j.count(T, T))
                sp.dma_start(out_rows[j.number()], y_sb[:, j.par]).then_inc(out_stored[j.par], 16)

            def turn(i):
                peeled = isinstance(i.m, int)
                if not peeled or i.off + 2 < PAIRS:
                    load_x(i.plus(2))
                if not peeled or i.off + 1 < PAIRS:
                    load_adj(i.plus(1))
                if not peeled or i.off >= 1:
                    load_resid(i.plus(-1))
                if not peeled or i.off >= 2:
                    store(i.plus(-2))

            load_x(Pair(0, 0))
            sp.dma_start(w_raw[WK], weights[WK]).then_inc(w_loaded[WK], 16)
            for column, bias in ((bq_col, bq), (bk_col, bk), (bv_col, bv)):
                sp.dma_start(column[:], bias.rearrange("(c p) -> p c", p=P),
                             allow_slow_non_contiguous=True).then_inc(bias_loaded, 16)
            sp.dma_start(bf_row[:], bf.partition_broadcast(P)).then_inc(bias_loaded, 16)
            sp.dma_start(w_raw[WV], weights[WV]).then_inc(w_loaded[WV], 16)
            load_adj(Pair(0, 0))
            load_x(Pair(0, 1))
            sp.dma_start(w_raw[WF], weights[WF]).then_inc(w_loaded[WF], 16)
            for n in range(4):
                sp.wait_ge(w_ready[n], 1)
            turns(sp, turn)
            last = Pair(0, PAIRS - 1)
            store(last.plus(-1))
            for t in range(T):
                sp.wait_ge(normed, last.count(T, t + 1))
                sp.dma_start(out_rows[PAIRS - 1][:, t], y_sb[:, last.par, t]).then_inc(last_stored, 16)
            for par in range(2):
                sp.wait_ge(out_stored[par], 16 * (PAIRS // 2 - par))
            sp.wait_ge(last_stored, 16 * T)

        @block.gpsimd
        def _(pool):
            def build_mask(j, g):
                hold(pool, masked, j.plus(-2).count(UNITS * TILES, UNITS * TILES))
                if g == 0:
                    hold(pool, adj_loaded[j.par], j.dma())
                rows = slice(g * QT, (g + 1) * QT)
                nc.gpsimd.tensor_scalar(mask[:, j.par, rows], adj_raw[:, j.par, rows], -NEG / SCALE, NEG / SCALE,
                                        ALU.mult, ALU.add).then_inc(mask_built, 1)

            def scale_probs(i, u):
                hold(pool, inv_ready, i.count(UNITS, u + 1))
                for k in range(TILES):
                    tile = probs[:, u % 2, k]
                    at = u * TILES + k
                    nc.gpsimd.tensor_scalar(tile, tile, inv_col[:, at:at + 1], 1.0, ALU.mult,
                                            ALU.mult).then_inc(scaled, 1)

            def split_low(n):
                pool.wait_ge(w_high_ready, n + 1)
                nc.gpsimd.tensor_tensor(w_low[:, n], w_raw[n], w_high[:, n].bitcast(F32),
                                        ALU.subtract).then_inc(w_ready[n], 1)

            def add_bias(j, t):
                if t == 0:
                    pool.wait_ge(resid_loaded, j.m * 32 + (j.off * 16 + 16))
                nc.gpsimd.tensor_tensor(resid[:, t], resid[:, t], bf_row[:], ALU.add).then_inc(resid_ready, 1)

            def add_bias_last(t):
                tile = x_raw[:, (PAIRS - 1) % 2, t]
                nc.gpsimd.tensor_tensor(tile, tile, bf_row[:], ALU.add).then_inc(resid_ready, 1)

            def make_rstd(j, tiles=slice(0, T), done=1):
                hold(pool, var_ready, j.count(T, tiles.stop))
                nc.gpsimd.tensor_scalar(var_eps[:, tiles], mean_var[:, tiles, 1], EPS, None,
                                        ALU.add).then_inc(eps_added, 1)
                hold(pool, eps_added, j.count(1, done))
                nc.gpsimd.tensor_tensor(rstd[:, tiles], var_eps[:, tiles], neg_half[:, tiles],
                                        ALU.pow).then_inc(rstd_ready, 1)

            def turn(i):
                peeled = isinstance(i.m, int)
                for u in range(UNITS):
                    if u == 4 and (not peeled or i.off >= 2):
                        make_rstd(i.plus(-2))
                    scale_probs(i, u)
                    if u < 2 and (not peeled or i.off + 1 < PAIRS):
                        build_mask(i.plus(1), u)
                    at = 1 if peeled and i.off == PAIRS - 1 else 2
                    if u in (at, at + 1) and (not peeled or i.off >= 1):
                        add_bias(i.plus(-1), 2 * (u - at))
                        add_bias(i.plus(-1), 2 * (u - at) + 1)
                    if at == 1 and u in (3, 4):
                        if u == 3:
                            pool.wait_ge(x_turned, i.count(C, C))
                        add_bias_last(2 * u - 6)
                        add_bias_last(2 * u - 5)

            nc.gpsimd.memset(ident[:], 0.0).then_inc(ident_zero, 1)
            nc.gpsimd.memset(neg_half[:], -0.5).then_inc(const_ready, 1)
            pool.wait_ge(ident_zero, 1)
            nc.gpsimd.affine_select(out=ident[:], in_=ident[:], compare_op=ALU.not_equal, fill=1.0, base=0,
                                    pattern=[[-1, P]], channel_multiplier=1).then_inc(const_ready, 1)
            pool.wait_ge(const_ready, 2)
            for g in range(2):
                build_mask(Pair(0, 0), g)
            split_low(WV)
            pool.wait_ge(bias_loaded, 64)
            turns(pool, turn)
            last = Pair(0, PAIRS - 1)
            make_rstd(last.plus(-1))
            make_rstd(last, slice(0, 2), 1)
            make_rstd(last, slice(2, 4), 2)

        @block.scalar
        def _(act):
            def split_weight(n):
                act.wait_ge(w_loaded[n], 16)
                nc.scalar.copy(w_high[:, n], w_raw[n]).then_inc(w_high_ready, 1)

            def exps(i, u):
                for k in range(TILES):
                    at = u * TILES + k
                    act.wait_ge(masked, i.count(UNITS * TILES, at + 1))
                    tile = probs[:, u % 2, k]
                    nc.scalar.activation(tile, tile, ACT.Exp, bias=low_col[:, at:at + 1], scale=-1.0,
                                         accum_out=sum_col[:, at:at + 1]).then_inc(exp_done, 1)

            def copy_turned(i, u):
                wait(act, pv_done, i.count(UNITS, u - 1))
                for h in range(2):
                    act.wait_ge(p_turned, i.count(2 * UNITS, 2 * u + h + 1))
                    nc.scalar.copy(probs_t[:, u % 2, h], turned_bank[h][:]).then_inc(pt_ready, 1)

            def context_high(i, c):
                act.wait_ge(pv_done, i.count(UNITS, 2 * c + 2))
                nc.scalar.activation(ctx_high[:, i.par, c], ctx_bank[:], ACT.Identity,
                                     bias=bv_col[:, c:c + 1]).then_inc(ctx_high_ready, 1)

            def last_context_high(g):
                part = slice(g * S, (g + 1) * S)
                last = Pair(0, PAIRS - 1)
                act.wait_ge(pv_done, last.count(UNITS, 2 * C - 1 + g))
                nc.scalar.activation(ctx_high[:, last.par, C - 1, part], last_ctx_bank[g][:, part], ACT.Identity,
                                     bias=bv_col[:, C - 1:C]).then_inc(ctx_high_ready, 1)

            def take(kind, j, n, bank):
                if kind == "x":
                    act.wait_ge(x_turned, j.count(C, n + 1))
                    nc.scalar.copy(xt_high[:, n], proj_bank[bank][:]).then_inc(xt_high_ready, 1)
                elif kind == "q":
                    act.wait_ge(qk_done, j.count(2 * C, 2 * n + 1))
                    for h in range(2):
                        d = halves[h]
                        nc.scalar.activation(q_stack[d, j.par, n, h], proj_bank[bank][d, :], ACT.Identity,
                                             bias=bq_col[d, n:n + 1]).then_inc(qk_high_ready, 1)
                elif kind == "k":
                    act.wait_ge(qk_done, j.count(2 * C, 2 * n + 2))
                    nc.scalar.activation(k_high[:, j.par, n], proj_bank[bank][:], ACT.Identity,
                                         bias=bk_col[:, n:n + 1]).then_inc(qk_high_ready, 1)
                elif kind == "v":
                    act.wait_ge(v_done, j.count(T, n + 1))
                    nc.scalar.copy(v_sb[:, j.par, n], proj_bank[bank][:, 0:D]).then_inc(v_ready, 1)

            def turn(i):
                follows = not isinstance(i.m, int) or i.off >= 1
                for u in range(UNITS):
                    pieces = list(work(i, u))
                    if follows or u >= 2:
                        exps(i, u)
                    for piece in pieces[:1]:
                        take(*piece)
                    if u >= 2 or (u and follows):
                        copy_turned(i, u - 1)
                    elif follows:
                        copy_turned(i.plus(-1), UNITS - 1)
                    for piece in pieces[1:2]:
                        take(*piece)
                    if u in (3, 5):
                        context_high(i, u // 2 - 1)
                    if u == 1 and follows:
                        context_high(i.plus(-1), C - 1)
                    for piece in pieces[2:]:
                        take(*piece)

            act.dma_start(w_raw[WQ], weights[WQ]).then_inc(w_loaded[WQ], 16)
            take("x", Pair(0, 0), *FIRST[0][2:])
            split_weight(WQ)
            for kind, j, n, bank in FIRST[1:3]:
                take(kind, Pair(0, j), n, bank)
            split_weight(WK)
            act.wait_ge(bias_loaded, 64)
            for kind, j, n, bank in FIRST[3:7]:
                take(kind, Pair(0, j), n, bank)
            split_weight(WV)
            for kind, j, n, bank in FIRST[7:9]:
                take(kind, Pair(0, j), n, bank)
            first = Pair(0, 0)
            exps(first, 0)
            for kind, j, n, bank in FIRST[9:12]:
                take(kind, Pair(0, j), n, bank)
            split_weight(WF)
            for kind, j, n, bank in FIRST[12:]:
                take(kind, Pair(0, j), n, bank)
            copy_turned(first, 0)
            exps(first, 1)
            turns(act, turn)
            copy_turned(Pair(0, PAIRS - 1), UNITS - 1)
            for g in range(2):
                last_context_high(g)

        @block.vector
        def _(dve):
            def split_weight(n):
                dve.wait_ge(w_high_ready, n + 1)
                nc.vector.tensor_tensor(w_low[:, n], w_raw[n], w_high[:, n].bitcast(F32),
                                        ALU.subtract).then_inc(w_ready[n], 1)

            def mask_scores(i, u):
                if u == 0:
                    hold(dve, mask_built, i.count(2, 2))
                hold(dve, p_turned, i.count(2 * UNITS, 2 * (u - 1)))
                for k in range(TILES):
                    h, q = k // QT, k % QT
                    at = u * TILES + k
                    if q == 0:
                        hold(dve, scores_done, i.count(2 * UNITS, 2 * u + h + 1))
                    nc.vector.tensor_tensor_reduce(
                        out=probs[:, u % 2, k], in0=score_bank[(2 * u + h) % 3][:, q * S:(q + 1) * S],
                        in1=mask[:, i.par, (u % 2) * QT + q], scale=-SCALE, scalar=SMALLEST_START, op0=ALU.add,
                        op1=ALU.min, accum_out=low_col[:, at:at + 1]).then_inc(masked, 1)

            def invert_sums(i, u):
                dve.wait_ge(exp_done, i.count(UNITS * TILES, (u + 1) * TILES))
                cols = slice(u * TILES, (u + 1) * TILES)
                nc.vector.reciprocal(inv_col[:, cols], sum_col[:, cols]).then_inc(inv_ready, 1)

            def context_low(i, c):
                dve.wait_ge(ctx_high_ready, i.count(C, c + 1))
                nc.vector.scalar_tensor_tensor(out=ctx_low[:, i.par, c], in0=ctx_bank[:], scalar=bv_col[:, c:c + 1],
                                               in1=ctx_high[:, i.par, c].bitcast(F32), op0=ALU.add,
                                               op1=ALU.subtract).then_inc(ctx_ready, 1)

            def last_context_low(g):
                part = slice(g * S, (g + 1) * S)
                last = Pair(0, PAIRS - 1)
                dve.wait_ge(ctx_high_ready, last.count(C, C + g))
                nc.vector.scalar_tensor_tensor(out=ctx_low[:, last.par, C - 1, part],
                                               in0=last_ctx_bank[g][:, part],
                                               scalar=bv_col[:, C - 1:C],
                                               in1=ctx_high[:, last.par, C - 1, part].bitcast(F32), op0=ALU.add,
                                               op1=ALU.subtract).then_inc(ctx_ready, 1)

            def last_y(t):
                last = Pair(0, PAIRS - 1)
                if t == 0:
                    wait(dve, out_stored[last.par], last.plus(-2).dma())
                    dve.wait_ge(resid_ready, last.count(T, T))
                dve.wait_ge(o_done, last.count(T, t + 1))
                nc.vector.tensor_tensor(y_sb[:, last.par, t], proj_bank[LAST_BANKS[t]][:, 0:D],
                                        x_raw[:, last.par, t], ALU.add).then_inc(y_ready, 1)

            def take(kind, j, n, bank):
                if kind == "x":
                    dve.wait_ge(xt_high_ready, j.count(C, n + 1))
                    nc.vector.tensor_tensor(xt_low[:, n], proj_bank[bank][:], xt_high[:, n].bitcast(F32),
                                            ALU.subtract).then_inc(xt_ready, 1)
                elif kind == "q":
                    for h in range(2):
                        d, other = halves[h], halves[1 - h]
                        dve.wait_ge(qk_high_ready, j.count(3 * C, 3 * n + h + 1))
                        nc.vector.scalar_tensor_tensor(
                            out=q_stack[other, j.par, n, h], in0=proj_bank[bank][d, :], scalar=bq_col[d, n:n + 1],
                            in1=q_stack[d, j.par, n, h].bitcast(F32), op0=ALU.add,
                            op1=ALU.subtract).then_inc(qk_ready, 1)
                elif kind == "k":
                    dve.wait_ge(qk_high_ready, j.count(3 * C, 3 * n + 3))
                    for h in range(2):
                        d = halves[h]
                        nc.vector.scalar_tensor_tensor(
                            out=k_stack[d, j.par, n, h], in0=proj_bank[bank][d, :], scalar=bk_col[d, n:n + 1],
                            in1=k_high[d, j.par, n].bitcast(F32), op0=ALU.add,
                            op1=ALU.subtract).then_inc(qk_ready, 1)
                elif kind == "o":
                    if n == 0:
                        wait(dve, out_stored[j.par], j.plus(-2).dma())
                    dve.wait_ge(resid_ready, j.count(T, n + 1))
                    dve.wait_ge(o_done, j.count(T, n + 1))
                    nc.vector.tensor_tensor(y_sb[:, j.par, n], proj_bank[bank][:, 0:D], resid[:, n],
                                            ALU.add).then_inc(y_ready, 1)

            def shift_k(j, n):
                for h in range(2):
                    d, other = halves[h], halves[1 - h]
                    nc.vector.tensor_copy(k_stack[other, j.par, n, h],
                                          k_high[d, j.par, n].bitcast(F32)).then_inc(k_shifted, 1)

            def moments(j, tiles=range(T)):
                dve.wait_ge(y_ready, j.count(T, tiles[-1] + 1))
                for t in tiles:
                    nc.vector.bn_stats(stats[:, t], y_sb[:, j.par, t]).then_inc(stats_ready, 1)
                for t in tiles:
                    hold(dve, stats_ready, j.count(T, t + 1))
                    nc.vector.bn_aggr(mean_var[:, t], stats[:, t]).then_inc(var_ready, 1)

            def normalise(j, tiles=range(T), done=1):
                dve.wait_ge(rstd_ready, j.count(1, done))
                for t in tiles:
                    nc.vector.tensor_scalar(y_sb[:, j.par, t], y_sb[:, j.par, t], mean_var[:, t, 0:1],
                                            rstd[:, t:t + 1], ALU.subtract, ALU.mult).then_inc(normed, 1)

            def turn(i):
                peeled = isinstance(i.m, int)
                for u in range(UNITS):
                    pieces = list(work(i, u))
                    begun = peeled and i.off == 0 and u < 2
                    if not begun:
                        mask_scores(i, u)
                    if 1 <= u <= C and (not peeled or i.off + 1 < PAIRS):
                        shift_k(i.plus(1), u - 1)
                    if u == 5 and (not peeled or i.off >= 2):
                        normalise(i.plus(-2))
                    if not begun or u:
                        invert_sums(i, u)
                    if u == 3 and (not peeled or i.off >= 2):
                        moments(i.plus(-2))
                    for piece in pieces[:2]:
                        take(*piece)
                    if u in (3, 5):
                        context_low(i, u // 2 - 1)
                    if u == 1 and (not peeled or i.off >= 1):
                        context_low(i.plus(-1), C - 1)
                    for piece in pieces[2:]:
                        take(*piece)

            take("x", Pair(0, 0), *FIRST[0][2:])
            split_weight(WQ)
            for kind, j, n, bank in FIRST[1:3]:
                take(kind, Pair(0, j), n, bank)
            split_weight(WK)
            for kind, j, n, bank in FIRST[3:9]:
                take(kind, Pair(0, j), n, bank)
                if kind == "k":
                    shift_k(Pair(0, j), n)
            first = Pair(0, 0)
            mask_scores(first, 0)
            invert_sums(first, 0)
            split_weight(WF)
            for kind, j, n, bank in FIRST[9:]:
                take(kind, Pair(0, j), n, bank)
            mask_scores(first, 1)
            turns(dve, turn)
            last = Pair(0, PAIRS - 1)
            moments(last.plus(-1))
            last_context_low(0)
            normalise(last.plus(-1))
            last_context_low(1)
            for g in range(2):
                for t in (2 * g, 2 * g + 1):
                    last_y(t)
                moments(last, range(2 * g, 2 * g + 2))
            for g in range(2):
                normalise(last, range(2 * g, 2 * g + 2), g + 1)

        @block.tensor
        def _(pe):
            def split_product(bank_ap, terms, waits={}):
                for n, (stationary, moving) in enumerate(terms):
                    if n in waits:
                        pe.wait_ge(*waits[n])
                    last = nc.tensor.matmul(bank_ap, stationary, moving, start=(n == 0), stop=(n == len(terms) - 1))
                return last

            def scores(i, u):
                c, g = u // 2, u % 2
                banks = [score_bank[(2 * u + h) % 3] for h in range(2)]
                if g == 0:
                    pe.wait_ge(qk_ready, i.count(4 * C, 4 * c + 4))
                    pe.wait_ge(k_shifted, i.count(2 * C, 2 * c + 2))
                wait(pe, masked, i.count(UNITS * TILES, 2 * (2 * u + 1) - 4))
                keys = slice(g * S, (g + 1) * S)
                for q in range(QT):
                    rows = slice(g * S + q * P, g * S + (q + 1) * P)
                    for h in range(2):
                        nc.tensor.matmul(banks[h][:, q * S:(q + 1) * S], q_stack[:, i.par, c, h, rows],
                                         k_stack[:, i.par, c, h, keys], start=True, stop=False)
                    for h in range(2):
                        d = halves[h]
                        mm = nc.tensor.matmul(banks[h][:, q * S:(q + 1) * S], q_stack[d, i.par, c, h, rows],
                                              k_high[d, i.par, c, keys], start=False, stop=True)
                        if q == QT - 1:
                            mm.then_inc(scores_done, 1)

            def turn_probs(i, u):
                for h in range(2):
                    pe.wait_ge(scaled, i.count(UNITS * TILES, u * TILES + (h + 1) * QT))
                    wait(pe, pt_ready, i.count(2 * UNITS, 2 * (u - 1) + h + 1))
                    for q in range(QT):
                        for k in range(QT):
                            at = k * S + q * P
                            mm = nc.tensor.transpose(turned_bank[h][:, at:at + P],
                                                     probs[:, u % 2, h * QT + q, k * P:(k + 1) * P], ident[:])
                    mm.then_inc(p_turned, 1)

            def times_v(i, u, bank=ctx_bank):
                c, g = u // 2, u % 2
                if u == 0:
                    pe.wait_ge(v_ready, i.count(T, T))
                if g == 0:
                    wait(pe, ctx_ready, i.count(C, c))
                pe.wait_ge(pt_ready, i.count(2 * UNITS, 2 * u + 2))
                for k in range(QT):
                    for h in range(2):
                        d = halves[h]
                        feats = slice(c * P + h * HD, c * P + (h + 1) * HD)
                        mm = nc.tensor.matmul(bank[d, g * S:(g + 1) * S], v_sb[:, i.par, g * QT + k, feats],
                                              probs_t[:, u % 2, h, k * S:(k + 1) * S],
                                              start=(k == 0), stop=(k == QT - 1))
                mm.then_inc(pv_done, 1)

            def make(kind, j, n, bank):
                full = proj_bank[bank][:]
                tokens = slice(n * P, (n + 1) * P)
                if kind == "x":
                    if n == 0:
                        pe.wait_ge(x_loaded[j.par], j.dma())
                    for t in range(T):
                        mm = nc.tensor.transpose(full[:, t * P:(t + 1) * P], x_raw[:, j.par, t, tokens], ident[:])
                    mm.then_inc(x_turned, 1)
                elif kind in "qk":
                    w = WQ if kind == "q" else WK
                    terms = [term for a, b in ((w_high, xt_high), (w_high, xt_low), (w_low, xt_high))
                             for term in ((a[:, w, c, tokens], b[:, c]) for c in range(C))]
                    waits = {}
                    if kind == "q" and n == 0:
                        waits = {0: (xt_high_ready, j.count(C, C))}
                        for c in range(C):
                            waits[C + c] = (xt_ready, j.count(C, c + 1))
                    if isinstance(j.m, int) and j.off == 0 and n == 0:
                        pe.wait_ge(w_high_ready, w + 1)
                        waits[2 * C] = (w_ready[w], 1)
                    split_product(full, terms, waits).then_inc(qk_done, 1)
                elif kind == "v":
                    terms = [term for c in range(C) for term in (
                        (xt_high[:, c, tokens], w_high[:, WV, c]), (xt_high[:, c, tokens], w_low[:, WV, c]),
                        (xt_low[:, c, tokens], w_high[:, WV, c]))]
                    split_product(full[:, 0:D], terms).then_inc(v_done, 1)
                else:
                    if n == 0:
                        pe.wait_ge(ctx_ready, j.count(C, C))
                    terms = [term for c in range(C) for term in (
                        (ctx_high[:, j.par, c, tokens], w_high[:, WF, c]),
                        (ctx_high[:, j.par, c, tokens], w_low[:, WF, c]),
                        (ctx_low[:, j.par, c, tokens], w_high[:, WF, c]))]
                    split_product(full[:, 0:D], terms).then_inc(o_done, 1)

            def turn(i):
                peeled = isinstance(i.m, int)
                if peeled and i.off == PAIRS - 1:
                    held = {0: ("o", i.plus(-2), 3), 1: ("v", i, 0)}
                elif not peeled or i.off >= 2:
                    held = {0: ("o", i.plus(-2), 3), 1: ("o", i.plus(-2), 2)}
                elif i.off == 1:
                    held = {0: ("x", Pair(0, 2), 2), 1: ("x", Pair(0, 2), 1)}
                else:
                    held = {0: ("x", Pair(0, 1), 1), 1: ("x", Pair(0, 1), 2)}

                def make_next(pieces):
                    for kind, j, n, bank in pieces:
                        pe.wait_ge(*emptied(*held[bank]))
                        make(kind, j, n, bank)
                        held[bank] = (kind, j, n)

                if peeled and i.off == 1:
                    pe.wait_ge(w_ready[WF], 1)
                for u in range(UNITS):
                    pieces = list(work(i, u))
                    begun = peeled and i.off == 0 and u < 2
                    if not begun:
                        scores(i, u)
                    make_next(pieces[:1])
                    if u:
                        if not begun:
                            turn_probs(i, u - 1)
                    elif not peeled or i.off >= 1:
                        turn_probs(i.plus(-1), UNITS - 1)
                    make_next(pieces[1:2])
                    if u >= 2:
                        times_v(i, u - 2)
                    elif not peeled or i.off >= 1:
                        times_v(i.plus(-1), UNITS - 2 + u)
                    make_next(pieces[2:])

            pe.wait_ge(const_ready, 2)
            held = {}
            for kind, j, n, bank in FIRST:
                if bank in held:
                    pe.wait_ge(*emptied(*held[bank]))
                if (kind, n) == ("v", 0):
                    pe.wait_ge(w_ready[WV], 1)
                if (kind, n) == ("v", 0):
                    scores(Pair(0, 0), 0)
                make(kind, Pair(0, j), n, bank)
                held[bank] = (kind, Pair(0, j), n)
            scores(Pair(0, 0), 1)
            turn_probs(Pair(0, 0), 0)
            turns(pe, turn)

            last = Pair(0, PAIRS - 1)

            def last_o(t, chunks):
                tokens = slice(t * P, (t + 1) * P)
                for c in chunks:
                    for n, (stationary, moving) in enumerate((
                            (ctx_high[:, last.par, c, tokens], w_high[:, WF, c]),
                            (ctx_high[:, last.par, c, tokens], w_low[:, WF, c]),
                            (ctx_low[:, last.par, c, tokens], w_high[:, WF, c]))):
                        mm = nc.tensor.matmul(proj_bank[LAST_BANKS[t]][:, 0:D], stationary, moving,
                                              start=(c == 0 and n == 0), stop=(c == C - 1 and n == 2))
                if chunks[-1] == C - 1:
                    mm.then_inc(o_done, 1)

            pe.wait_ge(ctx_ready, last.count(C, 1))
            pe.wait_ge(y_ready, last.plus(-1).count(T, T - 1))
            last_o(0, [0])
            pe.wait_ge(masked, last.count(UNITS * TILES, UNITS * TILES))
            for t in range(1, T):
                last_o(t, [0])
            turn_probs(last, UNITS - 1)
            times_v(last, UNITS - 2)
            pe.wait_ge(ctx_ready, last.count(C, 2))
            for t in range(2):
                last_o(t, [1])
            pe.wait_ge(y_ready, last.plus(-1).count(T, T))
            times_v(last, UNITS - 1, last_ctx_bank[1])
            for t in range(2, T):
                last_o(t, [1])
            for t in range(T):
                if t % QT == 0:
                    pe.wait_ge(ctx_ready, last.count(C, C + t // QT))
                last_o(t, [C - 1])


_INS = ['x', 'adj', 'L0_gnn_Wq', 'L0_gnn_bq', 'L0_gnn_Wk', 'L0_gnn_bk', 'L0_gnn_Wv', 'L0_gnn_bv', 'L0_gnn_Wf',
        'L0_gnn_bf']


def kernel(**inputs):
    import numpy as _np
    import concourse.bacc as _bacc
    from concourse import mybir as _mybir
    from concourse.bass_utils import run_bass_kernel_spmd as _run

    nc = _bacc.Bacc("TRN2", target_bir_lowering=False, num_devices=1)
    arrays, args = {}, []
    for name in _INS:
        a = _np.ascontiguousarray(inputs[name])
        arrays[f"in_{name}_dram"] = a
        args.append(nc.dram_tensor(f"in_{name}_dram", a.shape, _mybir.dt.from_np(a.dtype), kind="ExternalInput").ap())
    args.append(nc.dram_tensor("out_0_dram", inputs["x"].shape, _mybir.dt.float32, kind="ExternalOutput").ap())
    graph_attention(nc, *args)
    r = _run(nc, [arrays], core_ids=[0])
    return r.results[0]["out_0_dram"]
```
